# Optimizing a Trainium2 kernel written in Bass

```python
import numpy as np
import jax
import jax.numpy as jnp

def _softmax(x, axis=-1):
    return jax.nn.softmax(x, axis=axis)

def _gelu(x):
    return jax.nn.gelu(x, approximate=True)

def _silu(x):
    return jax.nn.silu(x)

def _sigmoid(x):
    return jax.nn.sigmoid(x)

def _layernorm(x, axis=-1, eps=1e-05):
    m = jnp.mean(x, axis=axis, keepdims=True)
    v = jnp.var(x, axis=axis, keepdims=True)
    return (x - m) / jnp.sqrt(v + eps)

def _scatter_add(tgt, idx, src, axis=0):
    return tgt.at[idx].add(src)

def _segment_sum(src, seg, n):
    return jax.ops.segment_sum(src, seg, n)
kernel_name = 'mk_early_fusion_d1_tok_img1024_r4_eeb9f0'

def setup_inputs(seed: int=0):
    np.random.seed(seed)
    _w = jnp.asarray

    def _rec_inputs():
        import jax
        import jax.numpy as jnp
        _rk = jax.random.key(seed)
        x = -0.00016672 + 0.999947 * jax.random.normal(jax.random.fold_in(_rk, 1), (64, 3, 224, 224), jnp.float32)
        txt = -6.7295e-12 + 0.999995 * jax.random.normal(jax.random.fold_in(_rk, 2), (64, 77, 256), jnp.float32)
        return (x, txt)
    x, txt = _rec_inputs()

    def _L0_tok_setup():
        import jax, jax.numpy as jnp
        import numpy as np
        EPS = 1e-05
        PH = PW = 16

        def _layernorm(x, g, b):
            mu = jnp.mean(x, axis=-1, keepdims=True)
            var = jnp.mean(jnp.square(x - mu), axis=-1, keepdims=True)
            return (x - mu) * jax.lax.rsqrt(var + EPS) * g + b
        key = jax.random.key(seed)
        k1, k2 = jax.random.split(key)
        B, C, H, W_ = (64, 3, 96, 96)
        patch_dim, input_dim = (C * PH * PW, 256)
        img = jax.random.normal(k1, (B, C, H, W_), dtype=jnp.float32)
        W = jax.random.normal(k2, (patch_dim, input_dim), dtype=jnp.float32) * patch_dim ** (-0.5)
        return {'img': img, 'ln1_g': jnp.ones((patch_dim,), jnp.float32), 'ln1_b': jnp.zeros((patch_dim,), jnp.float32), 'W': W, 'b': jnp.zeros((input_dim,), jnp.float32), 'ln2_g': jnp.ones((input_dim,), jnp.float32), 'ln2_b': jnp.zeros((input_dim,), jnp.float32)}
    _L0_tok_all = _L0_tok_setup()
    _L0_tok_in = {k: v for k, v in _L0_tok_all.items() if k in ('ln1_g', 'ln1_b', 'W', 'b', 'ln2_g', 'ln2_b')}
    del _L0_tok_all

    def _L0_attn_setup():
        import jax, jax.numpy as jnp
        import numpy as np
        import math
        N, S, E, H = (4, 1024, 256, 16)
        D = E // H
        key = jax.random.key(seed)
        ks = jax.random.split(key, 9)
        w = 1.0 / math.sqrt(E)
        mk = lambda k, shape: jax.random.normal(k, shape, jnp.float32) * w
        return {'x': jax.random.normal(ks[0], (N, S, E), jnp.float32), 'Wq': mk(ks[1], (E, E)), 'bq': mk(ks[2], (E,)), 'Wk': mk(ks[3], (E, E)), 'bk': mk(ks[4], (E,)), 'Wv': mk(ks[5], (E, E)), 'bv': mk(ks[6], (E,)), 'Wo': mk(ks[7], (E, E)), 'bo': mk(ks[8], (E,))}
    _L0_attn_all = _L0_attn_setup()
    _L0_attn_in = {k: v for k, v in _L0_attn_all.items() if k in ('Wq', 'bq', 'Wk', 'bk', 'Wv', 'bv', 'Wo', 'bo')}
    del _L0_attn_all

    def _L0_ffn_setup():
        import jax, jax.numpy as jnp
        import numpy as np
        DIM = 256

        def _reference_tuple_inner(x, W_r, W_k, W_v, mu_r, mu_k):
            B, T, C = x.shape
            x_prev = jnp.concatenate([jnp.zeros((B, 1, C), x.dtype), x[:, :-1, :]], axis=1)
            xr = mu_r * x + (1.0 - mu_r) * x_prev
            xk = mu_k * x + (1.0 - mu_k) * x_prev
            r = jax.nn.sigmoid(jnp.einsum('btc,dc->btd', xr, W_r))
            k = jnp.einsum('btc,dc->btd', xk, W_k)
            k_act = jnp.square(jax.nn.relu(k))
            out = r * jnp.einsum('btc,dc->btd', k_act, W_v)
            new_state = x[:, -1, :]
            return (out, new_state)
        key = jax.random.key(seed)
        ks = jax.random.split(key, 6)
        B, T, C = (8, 512, DIM)
        x = jax.random.normal(ks[0], (B, T, C), dtype=jnp.float32)
        s = 1.0 / np.sqrt(C)
        W_r = jax.random.uniform(ks[1], (C, C), jnp.float32, -s, s)
        W_k = jax.random.uniform(ks[2], (C, C), jnp.float32, -s, s)
        W_v = jax.random.uniform(ks[3], (C, C), jnp.float32, -s, s)
        mu_r = jax.random.uniform(ks[4], (C,), jnp.float32)
        mu_k = jax.random.uniform(ks[5], (C,), jnp.float32)
        return {'x': x, 'W_r': W_r, 'W_k': W_k, 'W_v': W_v, 'mu_r': mu_r, 'mu_k': mu_k}
    _L0_ffn_all = _L0_ffn_setup()
    _L0_ffn_in = {k: v for k, v in _L0_ffn_all.items() if k in ('W_r', 'W_k', 'W_v', 'mu_r', 'mu_k')}
    del _L0_ffn_all
    return {'x': x, 'txt': txt, 'L0_tok_ln1_g': _L0_tok_in['ln1_g'], 'L0_tok_ln1_b': _L0_tok_in['ln1_b'], 'L0_tok_W': _L0_tok_in['W'], 'L0_tok_b': _L0_tok_in['b'], 'L0_tok_ln2_g': _L0_tok_in['ln2_g'], 'L0_tok_ln2_b': _L0_tok_in['ln2_b'], 'L0_attn_Wq': _L0_attn_in['Wq'], 'L0_attn_bq': _L0_attn_in['bq'], 'L0_attn_Wk': _L0_attn_in['Wk'], 'L0_attn_bk': _L0_attn_in['bk'], 'L0_attn_Wv': _L0_attn_in['Wv'], 'L0_attn_bv': _L0_attn_in['bv'], 'L0_attn_Wo': _L0_attn_in['Wo'], 'L0_attn_bo': _L0_attn_in['bo'], 'L0_ffn_W_r': _L0_ffn_in['W_r'], 'L0_ffn_W_k': _L0_ffn_in['W_k'], 'L0_ffn_W_v': _L0_ffn_in['W_v'], 'L0_ffn_mu_r': _L0_ffn_in['mu_r'], 'L0_ffn_mu_k': _L0_ffn_in['mu_k']}

def reference(x, txt, L0_tok_ln1_g, L0_tok_ln1_b, L0_tok_W, L0_tok_b, L0_tok_ln2_g, L0_tok_ln2_b, L0_attn_Wq, L0_attn_bq, L0_attn_Wk, L0_attn_bk, L0_attn_Wv, L0_attn_bv, L0_attn_Wo, L0_attn_bo, L0_ffn_W_r, L0_ffn_W_k, L0_ffn_W_v, L0_ffn_mu_r, L0_ffn_mu_k):
    import jax
    import jax.numpy as jnp

    def _L0_tok_ref(img, ln1_g, ln1_b, W, b, ln2_g, ln2_b):
        import jax, jax.numpy as jnp
        import numpy as np
        EPS = 1e-05
        PH = PW = 16

        def _layernorm(x, g, b):
            mu = jnp.mean(x, axis=-1, keepdims=True)
            var = jnp.mean(jnp.square(x - mu), axis=-1, keepdims=True)
            return (x - mu) * jax.lax.rsqrt(var + EPS) * g + b
        B, C, H, Wd = img.shape
        x = img.reshape(B, C, H // PH, PH, Wd // PW, PW)
        x = jnp.transpose(x, (0, 2, 4, 3, 5, 1))
        x = x.reshape(B, -1, PH * PW * C)
        x = _layernorm(x, ln1_g, ln1_b)
        x = jnp.einsum('bnd,de->bne', x, W) + b
        x = _layernorm(x, ln2_g, ln2_b)
        return x

    def _L0_attn_ref(x, Wq, bq, Wk, bk, Wv, bv, Wo, bo):
        import jax, jax.numpy as jnp
        import numpy as np
        import math
        N, S, E, H = (4, 1024, 256, 16)
        D = E // H
        n, s, e = x.shape
        h, d = (H, D)
        scale = 1.0 / math.sqrt(d)

        def proj(W, b):
            y = jnp.einsum('nse,fe->nsf', x, W) + b
            return y.reshape(n, s, h, d).transpose(0, 2, 1, 3)
        Q = proj(Wq, bq)
        K = proj(Wk, bk)
        V = proj(Wv, bv)
        scores = jnp.einsum('nqhd,nkhd->nhqk', Q, K) * scale
        attn = jax.nn.softmax(scores, axis=-1)
        out = jnp.einsum('nhql,nlhd->nqhd', attn, V)
        out = out.reshape(n, s, e)
        return jnp.einsum('nse,fe->nsf', out, Wo) + bo

    def _L0_ffn_ref(x, W_r, W_k, W_v, mu_r, mu_k):
        import jax, jax.numpy as jnp
        import numpy as np
        DIM = 256

        def _reference_tuple_inner(x, W_r, W_k, W_v, mu_r, mu_k):
            B, T, C = x.shape
            x_prev = jnp.concatenate([jnp.zeros((B, 1, C), x.dtype), x[:, :-1, :]], axis=1)
            xr = mu_r * x + (1.0 - mu_r) * x_prev
            xk = mu_k * x + (1.0 - mu_k) * x_prev
            r = jax.nn.sigmoid(jnp.einsum('btc,dc->btd', xr, W_r))
            k = jnp.einsum('btc,dc->btd', xk, W_k)
            k_act = jnp.square(jax.nn.relu(k))
            out = r * jnp.einsum('btc,dc->btd', k_act, W_v)
            new_state = x[:, -1, :]
            return (out, new_state)
        return _reference_tuple_inner(x, W_r, W_k, W_v, mu_r, mu_k)[0]
    h = _L0_tok_ref(x, L0_tok_ln1_g, L0_tok_ln1_b, L0_tok_W, L0_tok_b, L0_tok_ln2_g, L0_tok_ln2_b)
    h = jnp.concatenate([h, txt], axis=1)
    h = h + _L0_attn_ref(_layernorm(h, axis=-1), L0_attn_Wq, L0_attn_bq, L0_attn_Wk, L0_attn_bk, L0_attn_Wv, L0_attn_bv, L0_attn_Wo, L0_attn_bo)
    h = h + _L0_ffn_ref(_layernorm(h, axis=-1), L0_ffn_W_r, L0_ffn_W_k, L0_ffn_W_v, L0_ffn_mu_r, L0_ffn_mu_k)
    return h

_drawn_inputs = setup_inputs


def setup_inputs(seed=0):
    import zlib

    import numpy as np

    out = dict(_drawn_inputs(seed))
    spreads = {'L0_tok_ln1_g': (1.0, 0.2),
     'L0_tok_ln1_b': (0.0, 0.1),
     'L0_tok_b': (0.0, 0.1),
     'L0_tok_ln2_g': (1.0, 0.2),
     'L0_tok_ln2_b': (0.0, 0.1)}
    factors = {'L0_attn_bq': 3.132, 'L0_attn_bk': 2.919, 'L0_ffn_W_r': 2.736, 'L0_ffn_mu_r': 5.722}
    for name, (base, spread) in spreads.items():
        noise = np.random.default_rng([zlib.crc32(name.encode()), seed]).standard_normal(out[name].shape)
        drawn = base * np.exp(spread * noise) if base else spread * noise
        out[name] = jnp.asarray(drawn.astype(out[name].dtype))
    for name, factor in factors.items():
        out[name] = (out[name] * factor).astype(out[name].dtype)
    return out
```

```python
from contextlib import ExitStack

import concourse.bass as bass
from concourse import mybir

F32 = mybir.dt.float32
F32R = mybir.dt.float32r
ALU = mybir.AluOpType
ACT = mybir.ActivationFunctionType
AX = mybir.AxisListType

IMAGES, CH, SIDE = 64, 3, 224
PS = 16
GRID = SIDE // PS
PATCHES = GRID * GRID
HALF = PS // 2
XROWS = 2 * CH * GRID
KCH = 2 * CH
PDIM = KCH * 128
TXT = 77
T = PATCHES + TXT
TP = T + 1
E = 256
HEADS, HD = 16, 16
TT = 91
TILES = T // TT
LASTP = PATCHES - 2 * TT

GT = 8
GROUPS = 36
TG = GT * GROUPS
PARTS = [(0, 16), (16, 32), (32, 36)]
PARTJ = [(0, 1, 2, 3), (0, 1, 2, 3), (0, 1, 2)]
QKV = 3 * HD
NQ = HEADS * QKV // 2
EPS = 1e-5

SLOT = 32
AT = dict(
    load=-12, xcols=-2, stats=-2, x=[0, 2, 4], tok=[6, 8], sums=5, stat=9, rstd1=10, txt=5, y=[11, 12, 13],
    rstd2=14, h=15, bn3=16, rstd3=17, xn=18, xt=[19, 20], qkv=[21, 23, 25, 27, 29, 31], hb=28,
    qkv_out=[25, 29, 33], qkv_in=36, spread=42, s=[51, 54, 57], pt=3, pv=5,
    o_in=68, ont=[72, 73], wo=[75, 77, 79], rstd4=81, z=82, zt=[84, 85], mix=87, k=[92, 94],
    r=[96, 97, 98], val=[99, 101, 103])

XCUT = [(0, 5), (5, 10), (10, 14)]


def images(slot, slot_parity, step, offset):
    if (step - offset) % SLOT == 0:
        back = (step - offset) // SLOT
        n = slot + back
        if not isinstance(slot, int) or 0 <= n < IMAGES:
            yield n, (slot_parity + back) % 2


class Signal:

    def __init__(self, ctx, nc, name, per, primed=False, unit=1):
        self.sem = ctx.enter_context(nc.semaphore(name))
        self.per, self.unit = per * unit, unit
        self.base = 2 * self.per if primed else 0

    def wait(self, eng, n, count):
        eng.wait_ge(self.sem, n * self.per + (self.base + count * self.unit))

    def done(self, ins):
        ins.then_inc(self.sem, self.unit)
        return ins


def fusion_kernel(nc, x, txt, ln1_g, ln1_b, tok_w, tok_b, ln2_g, ln2_b, wq, bq, wk, bk, wv, bv, wo, bo,
                  w_r, w_k, w_v, mu_r, mu_k, out):
    with ExitStack() as ctx:
        def sb(name, shape, dt=F32):
            return ctx.enter_context(nc.sbuf_tensor(name, shape, dt))

        def sig(name, per, primed=False, unit=1):
            return Signal(ctx, nc, name, per, primed, unit)

        ident = sb("ident", [128, 128])
        ones = sb("ones", [128, 128])
        rowmask = sb("rowmask", [XROWS, GRID])
        tokmask = sb("tokmask", [128, GT])
        g2b, b2b, c0b, bob = (sb(n, [128, E]) for n in ("g2b", "b2b", "c0b", "bob"))
        bqkv = sb("bqkv", [128, HEADS, QKV])
        mus = sb("mus", [128, 2, 2])
        small = sb("small", [128, 16])
        epst, powt = small[:, 0:TILES], small[:, 8:8 + TILES]
        wtok = sb("wtok", [128, 2, KCH, E], F32R)
        wqkv = sb("wqkv", [128, 2, 2, HEADS * QKV], F32R)
        wmat = {n: sb(n, [128, 2, 2, E], F32R) for n in ("woT", "wrT", "wkfT", "wvfT")}

        xim = sb("xim", [XROWS, HALF * SIDE])
        xcols = sb("xcols", [XROWS, GRID * 128])
        xst = sb("xst", [XROWS, GRID, 6])
        xs = sb("xs", [XROWS, 2, GRID])
        xtmp = sb("xtmp", [XROWS, 2, GRID])
        xspread = sb("xspread", [XROWS, 2, GRID, GRID])
        xT = sb("xT", [128, 2, KCH * GRID, GRID], F32R)
        stat1 = sb("stat1", [TT, TILES, 2])
        var1 = sb("var1", [TT, 2, TILES])
        rstd1 = sb("rstd1", [TT, TILES])
        yT = sb("yT", [128, 2, PATCHES])
        bn2, bn3, bn4 = (sb(n, [TT, TILES, 6]) for n in ("bn2", "bn3", "bn4"))
        mv2, mv3, mv4 = (sb(n, [TT, TILES, 2]) for n in ("mv2", "mv3", "mv4"))
        ve2, ve3, ve4 = (sb(n, [TT, TILES]) for n in ("ve2", "ve3", "ve4"))
        rs2, rs3, rs4 = (sb(n, [TT, TILES]) for n in ("rs2", "rs3", "rs4"))
        yxn = sb("yxn", [TT, TILES, E])
        h = sb("h", [TT, TILES, E])
        hb = sb("hb", [TT, 2, TILES, E])
        xnT = xT[:, :, :, :].rearrange("p a j w -> p (a j w)")[:, 0:4 * TP].rearrange("p (a k t) -> p a k t", a=2, k=2)
        qkvt = sb("qkvt", [TT, TILES, HEADS * QKV])

        qkv = sb("qkv", [128, GROUPS, QKV])
        kvb = sb("kvb", [128, GROUPS, GT, 2 * HD])
        probs = sb("probs", [128, 2, 4, GT, HD])
        mx = sb("mx", [128, 2, 4 * GT])
        rsum = sb("rsum", [128, 2, 4 * GT])
        probsT = sb("probsT", [128, 2, 4, 128])
        osb = sb("osb", [128, 9, 128])

        on = sb("on", [TT, TILES, E])
        onT = sb("onT", [128, 2, 2, TP], F32R)
        h2 = sb("h2", [TT, TILES, E])
        z = sb("z", [TT, TILES, E])
        zT = sb("zT", [128, 2, TP])
        dT = sb("dT", [128, 2, TP])
        mixf = sb("mixf", [128, 4, TP])
        mixp = sb("mixp", [128, 2, 2, 2, TP], F32R)
        kr = sb("kr", [128, 2, TP])
        kaf = sb("kaf", [128, 2, TP])
        kaT = sb("kaT", [128, 2, 2, TP], F32R)
        r = sb("r", [TT, TILES, E])
        rv = sb("rv", [TT, TILES, E])

        def bank(name):
            return ctx.enter_context(nc.psum_tensor(name, [128, 512], F32))

        s_ps = [bank("s_ps0"), bank("s_ps1")]
        f_ps = [bank("f_ps0"), bank("f_ps1")]
        t_ps = [bank("t_ps0"), bank("t_ps1")]
        pt_ps, o_ps = bank("pt_ps"), bank("o_ps")

        qkv_dram = nc.dram_tensor("qkv_dram", (TG, HEADS, QKV), F32, kind="Internal").ap()
        o_dram = nc.dram_tensor("o_dram", (HEADS, T, HD), F32, kind="Internal").ap()

        raw_in = ctx.enter_context(nc.semaphore("raw_in"))
        prep_pe = ctx.enter_context(nc.semaphore("prep_pe"))
        prep_dve = ctx.enter_context(nc.semaphore("prep_dve"))
        prep_pool = ctx.enter_context(nc.semaphore("prep_pool"))
        ready = ctx.enter_context(nc.semaphore("ready"))
        settled = ctx.enter_context(nc.semaphore("settled"))

        def settle(eng):
            eng.sem_inc(settled, 1)

        x_in = sig("x_in", 2, unit=16)
        txt_in = sig("txt_in", 1, unit=16)
        x_stats = sig("x_stats", 1, True)
        sums_pool = sig("sums_pool", 8, True)
        x_cols = sig("x_cols", 3, True)
        x_tr = sig("x_tr", 3, True)
        x_hi = sig("x_hi", 3)
        x_lo = sig("x_lo", 3)
        stat_pe = sig("stat_pe", 1, True)
        stat_sb = sig("stat_sb", 2)
        rstd1_pool = sig("rstd1_pool", 5)
        tok_pe = sig("tok_pe", 2, True)
        yT_sb = sig("yT_sb", 2)
        y_pe = sig("y_pe", 3, True)
        y_sb = sig("y_sb", 3, True)
        st2 = sig("st2", 3)
        mv2_sb = sig("mv2_sb", 3)
        rs2_pool = sig("rs2_pool", 2)
        hg = sig("hg", 3)
        h_sb = sig("h_sb", 3)
        st3 = sig("st3", 3)
        mv3_sb = sig("mv3_sb", 3)
        rs3_pool = sig("rs3_pool", 2)
        xn_sb = sig("xn_sb", 3)
        xn_pe = sig("xn_pe", 2, True)
        xn_hi = sig("xn_hi", 2)
        xn_lo = sig("xn_lo", 2)
        qkv_pe = sig("qkv_pe", 6, True)
        qkv_sb = sig("qkv_sb", 6, True)
        qkv_out = [sig(f"qkv_out{c}", 1, True, unit=16) for c in range(TILES)]
        qkv_in = sig("qkv_in", 1, True, unit=16)
        hb_sb = sig("hb_sb", 1, True)
        kvb_sb = sig("kvb_sb", 8, True)
        s_pe = sig("s_pe", 3, True)
        mx_sb = sig("mx_sb", 3)
        s_sub = sig("s_sub", 3, True)
        p_exp = sig("p_exp", 3)
        p_sum = sig("p_sum", 3, True)
        rsum_sb = sig("rsum_sb", 3)
        pt_pe = sig("pt_pe", 3, True)
        pt_sb = sig("pt_sb", 3, True)
        av_pe = sig("av_pe", 3, True)
        o_sb = sig("o_sb", 3, True)
        o_out = [sig(f"o_out{p}", len(PARTJ[p]), True, unit=16) for p in range(3)]
        on_in = sig("on_in", 1, True, unit=16)
        on_pe = sig("on_pe", 2, True)
        on_hi = sig("on_hi", 2)
        on_lo = sig("on_lo", 2)
        wo_pe = sig("wo_pe", 3, True)
        h2_sb = sig("h2_sb", 3, True)
        st4 = sig("st4", 3)
        mv4_sb = sig("mv4_sb", 3)
        rs4_pool = sig("rs4_pool", 2)
        z_sb = sig("z_sb", 3)
        z_pe = sig("z_pe", 2, True)
        zT_sb = sig("zT_sb", 2)
        d_sb = sig("d_sb", 2)
        mix_sb = sig("mix_sb", 4, True)
        mix_hi = sig("mix_hi", 4)
        mix_lo = sig("mix_lo", 4, True)
        k_pe = sig("k_pe", 2, True)
        kr_sb = sig("kr_sb", 2)
        ka_sb = sig("ka_sb", 2, True)
        ka_hi = sig("ka_hi", 2)
        ka_lo = sig("ka_lo", 2, True)
        r_pe = sig("r_pe", 3, True)
        r_tanh = sig("r_tanh", 3)
        val_pe = sig("val_pe", 3, True)
        rv_sb = sig("rv_sb", 3, True)
        out_sb = sig("out_sb", 3, True)
        out_dma = sig("out_dma", 3, True, unit=16)
        primed = [s for s in locals().values() if isinstance(s, Signal) and s.base] + qkv_out + o_out

        F_READ = ([(x_lo, 1), (x_lo, 2), (x_lo, 3), (yT_sb, 1), (yT_sb, 2), (stat_sb, 2), (y_sb, 1), (y_sb, 2),
                   (y_sb, 3), (xn_lo, 1), (xn_lo, 2)] + [(qkv_sb, j) for j in range(1, 7)])
        T_READ = [(on_lo, 1), (on_lo, 2), (h2_sb, 1), (h2_sb, 2), (h2_sb, 3), (zT_sb, 1), (zT_sb, 2), (kr_sb, 1),
                  (kr_sb, 2), (r_tanh, 1), (r_tanh, 2), (r_tanh, 3), (rv_sb, 1), (rv_sb, 2), (rv_sb, 3)]
        F_X, F_TOK, F_STAT, F_Y, F_XT, F_QKV = 0, 3, 5, 6, 9, 11
        T_ON, T_WO, T_ZT, T_K, T_R, T_VAL = 0, 2, 5, 7, 9, 12

        block = ctx.enter_context(nc.Block())

        FIRST, LAST, END = 3, 63, 67

        def slots(eng, body):
            for slot in range(-1, FIRST):
                body(slot, slot % 2)
            with eng.Fori(0, (LAST - FIRST) // 2) as i:
                for u in range(2):
                    body(i * 2 + (FIRST + u), (FIRST + u) % 2)
            for slot in range(LAST, END):
                body(slot, slot % 2)

        flat = kvb[:, :, :, :].rearrange("p g t c -> p (g t c)")
        raw = flat[:, 0:PDIM // 128 * E].rearrange("p (c e) -> p c e", c=KCH)
        c0rep = flat[:, 1536:1536 + PDIM].rearrange("p (c m) -> p c m", c=KCH)
        bnat = flat[:, 2304:2304 + 3 * E].rearrange("p (x e) -> p x e", x=3)
        lnt = flat[:, 3072:3084]
        WEIGHTS = [wq, wk, wv, wo, w_r, w_k, w_v]
        rawsq = flat[:, 3584:3584 + 7 * 2 * E].rearrange("p (n a e) -> p n a e", n=7, a=2)
        DVE_TOK = KCH + 1 + KCH + 1 + KCH + 2
        RAWS = 4 + 2 + 7 + 2 + 7 + 1

        @block.sync
        def _(sp):
            with nc.allow_non_contiguous_dma(reason="small vectors, once"):
                for c in range(2):
                    sp.dma_start(lnt[:, 3 * c:3 * c + 3], ln1_g[384 * c:384 * c + 384].rearrange("(p c) -> p c", c=CH)).then_inc(raw_in, 16)
                    sp.dma_start(lnt[:, 6 + 3 * c:9 + 3 * c], ln1_b[384 * c:384 * c + 384].rearrange("(p c) -> p c", c=CH)).then_inc(raw_in, 16)
                for s, v in ((0, mu_k), (1, mu_r)):
                    sp.dma_start(mus[:, s, :], v.rearrange("(k p) -> p k", p=128)).then_inc(raw_in, 16)
                for dst, v in ((g2b[:, :], ln2_g), (b2b[:, :], ln2_b), (c0b[:, :], tok_b), (bob[:, :], bo),
                               (bnat[:, 0, :], bq), (bnat[:, 1, :], bk), (bnat[:, 2, :], bv)):
                    sp.dma_start(dst, v.rearrange("(a e) -> a e", a=1).broadcast_to((128, E))).then_inc(raw_in, 16)
            for half in range(2):
                sp.dma_start(raw[:, 3 * half:3 * half + 3, :],
                             tok_w[384 * half:384 * half + 384, :].rearrange("(p c) e -> p c e", c=CH)).then_inc(raw_in, 16)
            for n, w in enumerate(WEIGHTS):
                sp.dma_start(rawsq[:, n, :, :], w.rearrange("(a p) e -> p a e", p=128)).then_inc(raw_in, 16)
            sp.wait_ge(prep_pool, 1)
            sp.dma_start(qkv_dram[T:TG, :, :].rearrange("t i j -> t (i j)"), qkvt[0:TG - T, 0, :]).then_inc(raw_in, 16)

            def after(signal, n, count):
                signal.wait(sp, n, count)
                settle(sp)

            def body(slot, par):
                for s in range(SLOT):
                    for n, p in images(slot, par, s, AT["load"]):
                        after(x_cols, n - 1, 3)
                        after(x_stats, n - 1, 1)
                        for half in range(2):
                            src = x[bass.ds(n, 1), :, :, :].rearrange("b c (i r) w -> (b c i) (r w)", r=PS)
                            x_in.done(sp.dma_start(xim[half * 42:half * 42 + 42, :],
                                                   src[:, half * HALF * SIDE:(half + 1) * HALF * SIDE]))
                    for n, p in images(slot, par, s, AT["txt"]):
                        after(hb_sb, n - 1, 1)
                        txt_in.done(sp.dma_start(h[LASTP:TT, 2, :], txt[bass.ds(n, 1), :, :].rearrange("b t e -> (b t) e")))
                    for c in range(TILES):
                        for n, p in images(slot, par, s, AT["qkv_out"][c]):
                            after(qkv_sb, n, 2 * c + 2)
                            if c == 0:
                                after(qkv_in, n - 1, 1)
                            qkv_out[c].done(sp.dma_start(qkv_dram[TT * c:TT * c + TT, :, :].rearrange("t i j -> t (i j)"), qkvt[:, c, :]))
                    for n, p in images(slot, par, s, AT["qkv_in"]):
                        for c in range(TILES):
                            after(qkv_out[c], n, 1)
                        after(kvb_sb, n - 1, 8)
                        after(s_pe, n - 1, 3)
                        qkv_in.done(sp.dma_start(qkv[:, :, :], qkv_dram.rearrange("(g t) i j -> (t i) g j", t=GT)))
                    for part in range(3):
                        for n, p in images(slot, par, s, AT["s"][part] + 7):
                            after(o_sb, n, part + 1)
                            if part == 0:
                                after(on_in, n - 1, 1)
                            for j in PARTJ[part]:
                                if part < 2:
                                    dst = o_dram[:, 128 * part:128 * part + 128, :].rearrange("q (b j t) d -> q j b (t d)", b=4, j=4)
                                    o_out[part].done(sp.dma_start(dst[:, j, :, :], osb[32 * j:32 * j + HEADS, 4 * part:4 * part + 4, :]))
                                else:
                                    t0 = 256 + GT * j
                                    t1 = min(t0 + GT, T)
                                    o_out[part].done(sp.dma_start(o_dram[:, t0:t1, :].rearrange("q t d -> q (t d)"),
                                                                  osb[32 * j:32 * j + HEADS, 8, 0:HD * (t1 - t0)]))
                    for n, p in images(slot, par, s, AT["o_in"]):
                        for part in range(3):
                            after(o_out[part], n, len(PARTJ[part]))
                        after(on_pe, n - 1, 2)
                        rows = o_dram.rearrange("q t d -> (q t d)").rearrange("(c p e) -> p c e", c=TILES, e=E)
                        on_in.done(sp.dma_start(on[:, :, :], rows))
                    for c in range(TILES):
                        for n, p in images(slot, par, s, AT["val"][c] + 3):
                            after(out_sb, n, c + 1)
                            o = out[bass.ds(n, 1), :, :].rearrange("b t e -> (b t) e")
                            out_dma.done(sp.dma_start(o[TT * c:TT * c + TT, :], h2[:, c, :]))

            slots(sp, body)
            out_dma.wait(sp, IMAGES - 1, 3)
            qkv_in.wait(sp, IMAGES - 1, 1)
            on_in.wait(sp, IMAGES - 1, 1)

        @block.gpsimd
        def _(pool):
            def prep(ins):
                ins.then_inc(prep_pool, 1)

            prep(nc.gpsimd.memset(qkvt[0:TG - T, 0, :], 0.0))
            prep(nc.gpsimd.memset(ident[:, :], 0.0))
            prep(nc.gpsimd.memset(tokmask[:, :], 1.0))
            prep(nc.gpsimd.memset(ones[:, :], 1.0))
            pool.wait_ge(prep_pool, 4)
            prep(nc.gpsimd.affine_select(out=ident[:, :], in_=ident[:, :], compare_op=ALU.not_equal, fill=1.0,
                                         base=0, pattern=[[-1, 128]], channel_multiplier=1))
            prep(nc.gpsimd.affine_select(out=tokmask[:, :], in_=tokmask[:, :], compare_op=ALU.is_ge, fill=0.0,
                                         base=0, pattern=[[-HD, GT]], channel_multiplier=1))
            pool.wait_ge(prep_pool, 6)
            prep(nc.gpsimd.affine_select(out=tokmask[:, :], in_=tokmask[:, :], compare_op=ALU.is_ge, fill=0.0,
                                         base=HD - 1, pattern=[[HD, GT]], channel_multiplier=-1))
            for k in range(KCH):
                src = ident[0:XROWS, GRID * k:GRID * k + GRID]
                if k == 0:
                    prep(nc.gpsimd.tensor_copy(rowmask[:, :], src))
                else:
                    prep(nc.gpsimd.tensor_tensor(rowmask[:, :], rowmask[:, :], src, ALU.add))
                pool.wait_ge(prep_pool, 8 + k)
            prep(nc.gpsimd.memset(small[:, 0:8], EPS))
            prep(nc.gpsimd.memset(small[:, 8:16], -0.5))
            zeroed = (stat1, mv2, zT, dT, mixf, kr)
            for t in zeroed:
                prep(nc.gpsimd.memset(t[:], 0.0))
            pool.wait_ge(prep_pool, 15 + len(zeroed))
            for s in primed:
                pool.sem_inc(s.sem, s.base)
            pool.wait_ge(ready, 1)

            def rsqrt(n, var, ve, rs, done):
                done.done(nc.gpsimd.tensor_tensor(ve, var, epst[0:TT, :], ALU.add))
                done.wait(pool, n, done.per - 1)
                done.done(nc.gpsimd.tensor_tensor(rs, ve, powt[0:TT, :], ALU.pow))

            def body(slot, par):
                for s in range(SLOT):
                    for n, p in images(slot, par, s, AT["sums"]):
                        me, mo, ve, vo = (xst[:, :, k] for k in (1, 4, 2, 5))
                        x_stats.wait(pool, n, 1)
                        stat_pe.wait(pool, n - 1, 1)
                        sums_pool.done(nc.gpsimd.tensor_tensor(xs[:, 0, :], me, mo, ALU.add))
                        sums_pool.done(nc.gpsimd.tensor_tensor(xs[:, 1, :], me, me, ALU.mult))
                        sums_pool.done(nc.gpsimd.tensor_tensor(xtmp[:, 0, :], mo, mo, ALU.mult))
                        sums_pool.done(nc.gpsimd.tensor_tensor(xtmp[:, 1, :], ve, vo, ALU.add))
                        sums_pool.wait(pool, n, 4)
                        sums_pool.done(nc.gpsimd.tensor_tensor(xs[:, 1, :], xs[:, 1, :], xtmp[:, 0, :], ALU.add))
                        sums_pool.done(nc.gpsimd.tensor_scalar(xtmp[:, 1, :], xtmp[:, 1, :], 2.0 / (HALF * PS), None, ALU.mult))
                        sums_pool.wait(pool, n, 6)
                        sums_pool.done(nc.gpsimd.tensor_tensor(xs[:, 1, :], xs[:, 1, :], xtmp[:, 1, :], ALU.add))
                        sums_pool.wait(pool, n, 7)
                        sums_pool.done(nc.gpsimd.tensor_tensor(
                            xspread[:, :, :, :].rearrange("p s i w -> p i s w"),
                            xs[:, :, :].unsqueeze(1).broadcast_to((XROWS, GRID, 2, GRID)),
                            rowmask[:, :].unsqueeze(2).unsqueeze(3).broadcast_to((XROWS, GRID, 2, GRID)), ALU.mult))
                    for n, p in images(slot, par, s, AT["rstd1"]):
                        stat_sb.wait(pool, n, 2)
                        y_sb.wait(pool, n - 1, 3)
                        settle(pool)
                        rstd1_pool.done(nc.gpsimd.tensor_scalar(var1[:, :, :].rearrange("p s c -> p c s"), stat1[:, :, :],
                                                                1.0 / (2 * KCH), None, ALU.mult))
                        rstd1_pool.wait(pool, n, 1)
                        rstd1_pool.done(nc.gpsimd.tensor_tensor(var1[:, 0, :], var1[:, 0, :], var1[:, 0, :], ALU.mult))
                        rstd1_pool.wait(pool, n, 2)
                        rstd1_pool.done(nc.gpsimd.tensor_tensor(var1[:, 1, :], var1[:, 1, :], var1[:, 0, :], ALU.subtract))
                        rstd1_pool.wait(pool, n, 3)
                        rstd1_pool.done(nc.gpsimd.tensor_tensor(var1[:, 0, :], var1[:, 1, :], epst[0:TT, :], ALU.add))
                        rstd1_pool.wait(pool, n, 4)
                        rstd1_pool.done(nc.gpsimd.tensor_tensor(rstd1[:, :], var1[:, 0, :], powt[0:TT, :], ALU.pow))
                    for n, p in images(slot, par, s, AT["rstd2"]):
                        mv2_sb.wait(pool, n, 3)
                        rsqrt(n, mv2[:, :, 1], ve2[:, :], rs2[:, :], rs2_pool)
                    for n, p in images(slot, par, s, AT["rstd3"]):
                        mv3_sb.wait(pool, n, 3)
                        rsqrt(n, mv3[:, :, 1], ve3[:, :], rs3[:, :], rs3_pool)
                    for n, p in images(slot, par, s, AT["hb"]):
                        h_sb.wait(pool, n, 3)
                        txt_in.wait(pool, n, 1)
                        h2_sb.wait(pool, n - 2, 3)
                        hb_sb.done(nc.gpsimd.tensor_tensor(hb[:, p, :, :], h[:, :, :],
                                                           bob[0:TT, :].unsqueeze(1).broadcast_to((TT, TILES, E)), ALU.add))
                    for n, p in images(slot, par, s, AT["rstd4"]):
                        mv4_sb.wait(pool, n, 3)
                        rsqrt(n, mv4[:, :, 1], ve4[:, :], rs4[:, :], rs4_pool)
                    for k in range(2):
                        for n, p in images(slot, par, s, AT["zt"][k] + 1):
                            zT_sb.wait(pool, n, k + 1)
                            mix_sb.wait(pool, n - 1, 4)
                            d_sb.done(nc.gpsimd.tensor_tensor(dT[:, k, 0:T], zT[:, k, 1:TP], zT[:, k, 0:T], ALU.subtract))
                    for j in range(4):
                        for n, p in images(slot, par, s, AT["mix"] + j + 1):
                            w, k = j // 2, j % 2
                            mix_hi.wait(pool, n, j + 1)
                            (r_pe if w else k_pe).wait(pool, n - 1, 3 if w else 2)
                            mix_lo.done(nc.gpsimd.tensor_tensor(mixp[:, w, 1, k, :], mixf[:, j, :],
                                                                mixp[:, w, 0, k, :].bitcast(F32), ALU.subtract))
                    for m in range(2):
                        for n, p in images(slot, par, s, AT["k"][m] + 1):
                            kr_sb.wait(pool, n, m + 1)
                            ka_lo.wait(pool, n - 1, 2)
                            ka_sb.done(nc.gpsimd.tensor_tensor(kaf[:, m, :], kr[:, m, :], kr[:, m, :], ALU.mult))
                        for n, p in images(slot, par, s, AT["k"][m] + 2):
                            ka_hi.wait(pool, n, m + 1)
                            val_pe.wait(pool, n - 1, 3)
                            ka_lo.done(nc.gpsimd.tensor_tensor(kaT[:, 1, m, :], kaf[:, m, :],
                                                               kaT[:, 0, m, :].bitcast(F32), ALU.subtract))
                    for c in range(TILES):
                        for n, p in images(slot, par, s, AT["val"][c] + 1):
                            rv_sb.wait(pool, n, c + 1)
                            out_sb.done(nc.gpsimd.tensor_tensor(h2[:, c, :], h2[:, c, :], rv[:, c, :], ALU.add))

            slots(pool, body)

        @block.vector
        def _(dve):
            V = nc.vector
            count = [0]

            def prep(ins):
                ins.then_inc(prep_dve, 1)
                count[0] += 1
                return count[0]

            dve.wait_ge(raw_in, RAWS * 16)
            dve.wait_ge(prep_pool, 6)
            wsum = yT[:, :, :].rearrange("p m t -> p (m t)")[:, 0:E]
            for ch in range(KCH):
                prep(V.tensor_scalar(c0rep[:, ch, :], ones[:, :], lnt[:, 6 + ch:7 + ch], None, ALU.mult))
            dve.wait_ge(prep_pe, 1)
            c = prep(V.tensor_tensor(c0b[:, :], f_ps[0][:, 0:E], c0b[:, :], ALU.add))
            for ch in range(KCH):
                c = prep(V.tensor_scalar(raw[:, ch, :], raw[:, ch, :], lnt[:, ch:ch + 1], None, ALU.mult))
            dve.wait_ge(prep_pe, 2)
            c = prep(V.tensor_scalar(wsum, t_ps[0][:, 0:E], 1.0 / PDIM, None, ALU.mult))
            dve.wait_ge(prep_dve, c)
            for ch in range(KCH):
                c = prep(V.tensor_tensor(raw[:, ch, :], raw[:, ch, :], wsum, ALU.subtract))
            dve.wait_ge(prep_dve, c)
            c = prep(V.tensor_copy(wtok[:, 0, :, :], raw))
            dve.wait_ge(prep_dve, c)
            c = prep(V.tensor_tensor(wtok[:, 1, :, :], raw, wtok[:, 0, :, :].bitcast(F32), ALU.subtract))
            assert c == DVE_TOK
            for n in range(len(WEIGHTS)):
                scale = {0: HD ** -0.5, 6: 0.5}.get(n, 1.0)
                dve.wait_ge(prep_pe, 3 + n)
                for k in range(2):
                    src = f_ps[n % 2][:, E * k:E * k + E]
                    if n < 3:
                        src = src.rearrange("p (h d) -> p d h", d=HD) if n < 2 else src.rearrange("p (h d) -> p h d", d=HD)
                        hi, lo = (wqkv[:, a, k, :].rearrange("p (i c) -> p i c", c=QKV)[:, :, HD * n:HD * n + HD] for a in range(2))
                    else:
                        hi, lo = (wmat[("woT", "wrT", "wkfT", "wvfT")[n - 3]][:, a, k, :] for a in range(2))
                    c = prep(V.tensor_scalar(hi, src, scale, None, ALU.mult))
                    dve.wait_ge(prep_dve, c)
                    c = prep(V.scalar_tensor_tensor(out=lo, in0=src, scalar=scale, in1=hi.bitcast(F32),
                                                    op0=ALU.mult, op1=ALU.subtract))
            for n in range(3):
                src = bnat[:, n, :].rearrange("p (h d) -> p d h", d=HD) if n < 2 else bnat[:, n, :].rearrange("p (h d) -> p h d", d=HD)
                c = prep(V.tensor_scalar(bqkv[:, :, HD * n:HD * n + HD], src, HD ** -0.5 if n == 0 else 1.0, None, ALU.mult))
            dve.wait_ge(prep_dve, c)
            dve.wait_ge(prep_pool, 21)
            dve.sem_inc(ready, 1)

            def norm_stats(n, src, c, bn, st, mv, mv_sb, rows=TT):
                st.done(V.bn_stats(bn[0:rows, c, :], src))
                st.wait(dve, n, c + 1)
                settle(dve)
                mv_sb.done(V.bn_aggr(mv[0:rows, c, :], bn[0:rows, c, :]))

            def body(slot, par):
                for s in range(SLOT):
                    for part, (g0, g1) in enumerate(PARTS):
                        nb = (g1 - g0) // 4
                        for n, p in images(slot, par, s, AT["s"][part] + 1):
                            b = (p + part) % 2
                            sc = s_ps[b][:, 0:128 * nb].rearrange("p (t k) -> p t k", k=HD)
                            s_pe.wait(dve, n, part + 1)
                            mx_sb.done(V.tensor_reduce(mx[:, b, 0:GT * nb], sc, AX.X, ALU.max))
                            mx_sb.wait(dve, n, part + 1)
                            if part >= 2:
                                pt_pe.wait(dve, n, part - 1)
                            else:
                                pt_pe.wait(dve, n - 1, part + 2)
                            s_sub.done(V.tensor_tensor(probs[:, b, 0:nb, :, :].rearrange("p b t k -> p (b t) k"), sc,
                                                       mx[:, b, 0:GT * nb].unsqueeze(2).broadcast_to((128, GT * nb, HD)), ALU.subtract))
                        for n, p in images(slot, par, s, AT["s"][part] + 3):
                            b = (p + part) % 2
                            p_exp.wait(dve, n, part + 1)
                            p_sum.done(V.tensor_reduce(rsum[:, b, 0:GT * nb], probs[:, b, 0:nb, :, :].rearrange("p b t k -> p (b t) k"), AX.X, ALU.add))
                            p_sum.wait(dve, n, part + 1)
                            rsum_sb.done(V.reciprocal(rsum[:, b, 0:GT * nb], rsum[:, b, 0:GT * nb]))
                        for n, p in images(slot, par, s, AT["s"][part] + 6):
                            b = (p + part) % 2
                            av_pe.wait(dve, n, part + 1)
                            rsum_sb.wait(dve, n, part + 1)
                            o_out[part].wait(dve, n - 1, len(PARTJ[part]))
                            o_sb.done(V.tensor_tensor(osb[:, 4 * part:4 * part + nb, :].rearrange("p b (t d) -> p (b t) d", d=HD),
                                                      o_ps[:, 0:128 * nb].rearrange("p (t d) -> p t d", d=HD),
                                                      rsum[:, b, 0:GT * nb].unsqueeze(2).broadcast_to((128, GT * nb, HD)), ALU.mult))
                    for k in range(7):
                        for n, p in images(slot, par, s, AT["stats"] + k):
                            if k == 0:
                                x_in.wait(dve, n, 2)
                                sums_pool.wait(dve, n - 1, 4)
                            for w in (2 * k, 2 * k + 1):
                                last = V.bn_stats(xst[:, w, :], xim[:, :].rearrange("p (r w) -> p r w", w=SIDE)[:, :, PS * w:PS * w + PS])
                            if k == 6:
                                x_stats.done(last)
                    for job, (w0, w1) in enumerate(XCUT):
                        for n, p in images(slot, par, s, AT["x"][job] + 1):
                            x_hi.wait(dve, n, job + 1)
                            src = f_ps[(p + F_X + job) % 2][:, 0:XROWS * (w1 - w0)].rearrange("p (w j) -> p j w", j=XROWS)
                            x_lo.done(V.tensor_tensor(xT[:, 1, :, w0:w1], src, xT[:, 0, :, w0:w1].bitcast(F32), ALU.subtract))
                    for n, p in images(slot, par, s, AT["stat"]):
                        stat_pe.wait(dve, n, 1)
                        src = f_ps[(p + F_STAT) % 2]
                        stat_sb.done(V.tensor_copy(stat1[:, 0:2, :], src[0:TT, 0:4].rearrange("p (c s) -> p c s", s=2)))
                        stat_sb.done(V.tensor_copy(stat1[0:LASTP, 2, :], src[0:LASTP, 4:6]))
                    for c in range(TILES):
                        rows = TT if c < 2 else LASTP
                        for n, p in images(slot, par, s, AT["y"][c] + 1):
                            y_pe.wait(dve, n, c + 1)
                            rstd1_pool.wait(dve, n, 5)
                            xn_pe.wait(dve, n - 1, 2)
                            y_sb.done(V.scalar_tensor_tensor(out=yxn[0:rows, c, :], in0=f_ps[(p + F_Y + c) % 2][0:rows, 0:E],
                                                             scalar=rstd1[0:rows, c:c + 1], in1=c0b[0:rows, :], op0=ALU.mult, op1=ALU.add))
                            y_sb.wait(dve, n, c + 1)
                            norm_stats(n, yxn[0:rows, c, :], c, bn2, st2, mv2, mv2_sb, rows)
                    for n, p in images(slot, par, s, AT["h"]):
                        rs2_pool.wait(dve, n, 2)
                        hb_sb.wait(dve, n - 1, 1)
                        for c in range(TILES):
                            rows = TT if c < 2 else LASTP
                            hg.done(V.scalar_tensor_tensor(out=yxn[0:rows, c, :], in0=yxn[0:rows, c, :], scalar=mv2[0:rows, c, 0:1],
                                                           in1=g2b[0:rows, :], op0=ALU.subtract, op1=ALU.mult))
                        for c in range(TILES):
                            rows = TT if c < 2 else LASTP
                            hg.wait(dve, n, c + 1)
                            h_sb.done(V.scalar_tensor_tensor(out=h[0:rows, c, :], in0=yxn[0:rows, c, :], scalar=rs2[0:rows, c:c + 1],
                                                             in1=b2b[0:rows, :], op0=ALU.mult, op1=ALU.add))
                    for n, p in images(slot, par, s, AT["bn3"]):
                        h_sb.wait(dve, n, 3)
                        txt_in.wait(dve, n, 1)
                        for c in range(TILES):
                            norm_stats(n, h[:, c, :], c, bn3, st3, mv3, mv3_sb)
                    for n, p in images(slot, par, s, AT["xn"]):
                        rs3_pool.wait(dve, n, 2)
                        for c in range(TILES):
                            xn_sb.done(V.tensor_scalar(yxn[:, c, :], h[:, c, :], mv3[:, c, 0:1], rs3[:, c:c + 1], ALU.subtract, ALU.mult))
                    for k in range(2):
                        for n, p in images(slot, par, s, AT["xt"][k] + 1):
                            xn_hi.wait(dve, n, k + 1)
                            xn_lo.done(V.tensor_tensor(xnT[:, 1, k, 0:T], f_ps[(p + F_XT + k) % 2][:, 0:T], xnT[:, 0, k, 0:T].bitcast(F32), ALU.subtract))
                    for job in range(6):
                        for n, p in images(slot, par, s, AT["qkv"][job] + 1):
                            c, half = job // 2, job % 2
                            qkv_pe.wait(dve, n, job + 1)
                            if half == 0:
                                qkv_out[c].wait(dve, n - 1, 1)
                            qkv_sb.done(V.tensor_tensor(qkvt[:, c, NQ * half:NQ * half + NQ], f_ps[(p + F_QKV + job) % 2][0:TT, 0:NQ],
                                                        bqkv[0:TT, :, :].rearrange("p i j -> p (i j)")[:, NQ * half:NQ * half + NQ], ALU.add))
                    for k in range(2):
                        for n, p in images(slot, par, s, AT["ont"][k] + 1):
                            on_hi.wait(dve, n, k + 1)
                            on_lo.done(V.tensor_tensor(onT[:, 1, k, 0:T], t_ps[(p + T_ON + k) % 2][:, 0:T], onT[:, 0, k, 0:T].bitcast(F32), ALU.subtract))
                    for c in range(TILES):
                        for n, p in images(slot, par, s, AT["wo"][c] + 1):
                            wo_pe.wait(dve, n, c + 1)
                            hb_sb.wait(dve, n, 1)
                            if c == 0:
                                out_dma.wait(dve, n - 1, 3)
                            h2_sb.done(V.tensor_tensor(h2[:, c, :], t_ps[(p + T_WO + c) % 2][0:TT, 0:E], hb[:, p, c, :], ALU.add))
                            h2_sb.wait(dve, n, c + 1)
                            norm_stats(n, h2[:, c, :], c, bn4, st4, mv4, mv4_sb)
                    for n, p in images(slot, par, s, AT["z"]):
                        rs4_pool.wait(dve, n, 2)
                        z_pe.wait(dve, n - 1, 2)
                        for c in range(TILES):
                            z_sb.done(V.tensor_scalar(z[:, c, :], h2[:, c, :], mv4[:, c, 0:1], rs4[:, c:c + 1], ALU.subtract, ALU.mult))
                    for j in range(4):
                        for n, p in images(slot, par, s, AT["mix"] + j):
                            w, k = j // 2, j % 2
                            d_sb.wait(dve, n, k + 1)
                            mix_lo.wait(dve, n - 1, j + 1)
                            mix_sb.done(V.scalar_tensor_tensor(out=mixf[:, j, 0:T], in0=dT[:, k, 0:T], scalar=mus[:, w, k:k + 1],
                                                               in1=zT[:, k, 0:T], op0=ALU.mult, op1=ALU.add))
                    for c in range(TILES):
                        for n, p in images(slot, par, s, AT["val"][c] + 1):
                            val_pe.wait(dve, n, c + 1)
                            r_tanh.wait(dve, n, c + 1)
                            out_sb.wait(dve, n - 1, c + 1)
                            rv_sb.done(V.scalar_tensor_tensor(out=rv[:, c, :], in0=r[:, c, :], scalar=1.0,
                                                              in1=t_ps[(p + T_VAL + c) % 2][0:TT, 0:E], op0=ALU.add, op1=ALU.mult))

            slots(dve, body)

        @block.scalar
        def _(act):
            A = nc.scalar
            act.wait_ge(ready, 1)

            def body(slot, par):
                for s in range(SLOT):
                    for t in range(GT):
                        for n, p in images(slot, par, s, AT["spread"] + t):
                            if t == 0:
                                qkv_in.wait(act, n, 1)
                                av_pe.wait(act, n - 1, 3)
                            kvb_sb.done(A.activation(kvb[:, :, t, :], qkv[:, :, HD:QKV], ACT.Copy, scale=tokmask[:, t:t + 1]))
                    for part, (g0, g1) in enumerate(PARTS):
                        nb = (g1 - g0) // 4
                        for n, p in images(slot, par, s, AT["s"][part] + 2):
                            b = (p + part) % 2
                            s_sub.wait(act, n, part + 1)
                            p_exp.done(A.activation(probs[:, b, 0:nb, :, :], probs[:, b, 0:nb, :, :], ACT.Exp))
                        for n, p in images(slot, par, s, AT["s"][part] + 4):
                            b = (p + part) % 2
                            pt_pe.wait(act, n, part + 1)
                            if part >= 2:
                                av_pe.wait(act, n, part - 1)
                            else:
                                av_pe.wait(act, n - 1, part + 2)
                            pt_sb.done(A.activation(probsT[:, b, 0:nb, :], pt_ps[:, 0:128 * nb], ACT.Copy))
                    for job, (w0, w1) in enumerate(XCUT):
                        for n, p in images(slot, par, s, AT["xcols"] + job):
                            if job == 0:
                                x_in.wait(act, n, 2)
                                x_tr.wait(act, n - 1, 3)
                            x_cols.done(A.activation(
                                xcols[:, 128 * w0:128 * w1].rearrange("p (w r q) -> p w r q", r=HALF, q=PS),
                                xim[:, :].rearrange("p (r w q) -> p w r q", r=HALF, q=PS)[:, w0:w1, :, :], ACT.Copy))
                        for n, p in images(slot, par, s, AT["x"][job] + 1):
                            x_tr.wait(act, n, job + 1)
                            if job == 0:
                                tok_pe.wait(act, n - 1, 2)
                                qkv_pe.wait(act, n - 1, 6)
                            src = f_ps[(p + F_X + job) % 2][:, 0:XROWS * (w1 - w0)].rearrange("p (w j) -> p j w", j=XROWS)
                            x_hi.done(A.activation(xT[:, 0, :, w0:w1], src, ACT.Copy))
                    for m in range(2):
                        for n, p in images(slot, par, s, AT["tok"][m] + 1):
                            tok_pe.wait(act, n, m + 1)
                            y_pe.wait(act, n - 1, 3)
                            yT_sb.done(A.activation(yT[:, m, :], f_ps[(p + F_TOK + m) % 2][:, 0:PATCHES], ACT.Copy))
                    for k in range(2):
                        for n, p in images(slot, par, s, AT["xt"][k] + 1):
                            xn_pe.wait(act, n, k + 1)
                            tok_pe.wait(act, n, 2)
                            xn_hi.done(A.activation(xnT[:, 0, k, 0:T], f_ps[(p + F_XT + k) % 2][:, 0:T], ACT.Copy))
                    for k in range(2):
                        for n, p in images(slot, par, s, AT["ont"][k] + 1):
                            on_pe.wait(act, n, k + 1)
                            wo_pe.wait(act, n - 1, 3)
                            on_hi.done(A.activation(onT[:, 0, k, 0:T], t_ps[(p + T_ON + k) % 2][:, 0:T], ACT.Copy))
                    for k in range(2):
                        for n, p in images(slot, par, s, AT["zt"][k] + 1):
                            z_pe.wait(act, n, k + 1)
                            mix_sb.wait(act, n - 1, 4)
                            zT_sb.done(A.activation(zT[:, k, 1:TP], t_ps[(p + T_ZT + k) % 2][:, 0:T], ACT.Copy))
                    for j in range(4):
                        for n, p in images(slot, par, s, AT["mix"] + j + 1):
                            w, k = j // 2, j % 2
                            mix_sb.wait(act, n, j + 1)
                            (r_pe if w else k_pe).wait(act, n - 1, 3 if w else 2)
                            mix_hi.done(A.activation(mixp[:, w, 0, k, :], mixf[:, j, :], ACT.Copy))
                    for m in range(2):
                        for n, p in images(slot, par, s, AT["k"][m] + 1):
                            k_pe.wait(act, n, m + 1)
                            ka_sb.wait(act, n - 1, m + 1)
                            kr_sb.done(A.activation(kr[:, m, 0:T], t_ps[(p + T_K + m) % 2][:, 0:T], ACT.Relu))
                        for n, p in images(slot, par, s, AT["k"][m] + 2):
                            ka_sb.wait(act, n, m + 1)
                            val_pe.wait(act, n - 1, 3)
                            ka_hi.done(A.activation(kaT[:, 0, m, :], kaf[:, m, :], ACT.Copy))
                    for c in range(TILES):
                        for n, p in images(slot, par, s, AT["r"][c] + 1):
                            r_pe.wait(act, n, c + 1)
                            rv_sb.wait(act, n - 1, 3)
                            r_tanh.done(A.activation(r[:, c, :], t_ps[(p + T_R + c) % 2][0:TT, 0:E], ACT.Tanh, scale=0.5))

            slots(act, body)

        @block.tensor
        def _(pe):
            mm, tr = nc.tensor.matmul, nc.tensor.transpose

            def product(psum, left, right):
                terms = [(a, b, k) for k in range(2) for a, b in ((0, 0), (0, 1), (1, 0))]
                for t, (a, b, k) in enumerate(terms):
                    last = mm(psum, left(a, k), right(b, k), start=t == 0, stop=t == len(terms) - 1)
                return last

            def turn(read, n, job):
                signal, value = read[job - 2]
                signal.wait(pe, n if job >= 2 else n - 1, value)

            pe.wait_ge(raw_in, RAWS * 16)
            pe.wait_ge(prep_pool, 6)
            pe.wait_ge(prep_dve, KCH)
            for ch in range(KCH):
                last = mm(f_ps[0][:, 0:E], c0rep[:, ch, :], raw[:, ch, :], start=ch == 0, stop=ch == KCH - 1)
            last.then_inc(prep_pe, 1)
            pe.wait_ge(prep_dve, 2 * KCH + 1)
            for ch in range(KCH):
                last = mm(t_ps[0][:, 0:E], ones[:, :], raw[:, ch, :], start=ch == 0, stop=ch == KCH - 1)
            last.then_inc(prep_pe, 1)
            for n in range(len(WEIGHTS)):
                if n >= 2:
                    pe.wait_ge(prep_dve, DVE_TOK + 4 * (n - 1))
                for k in range(2):
                    for a in range(2):
                        last = tr(f_ps[n % 2][:, E * k + 128 * a:E * k + 128 * a + 128], rawsq[:, n, a, 128 * k:128 * k + 128], ident[:, :])
                last.then_inc(prep_pe, 1)
            pe.wait_ge(ready, 1)

            def body(slot, par):
                for s in range(SLOT):
                    for part, (g0, g1) in enumerate(PARTS):
                        for n, p in images(slot, par, s, AT["s"][part]):
                            b = (p + part) % 2
                            if part == 0:
                                kvb_sb.wait(pe, n, 8)
                            if part >= 2:
                                s_sub.wait(pe, n, part - 1)
                            else:
                                s_sub.wait(pe, n - 1, part + 2)
                            for g in range(g0, g1):
                                row, j = (g - g0) // 4, g % 4
                                last = mm(s_ps[b][32 * j:32 * j + 32, 128 * row:128 * row + 128], qkv[:, g, 0:2 * HD],
                                          kvb[:, g, :, 0:HD], start=True, stop=True)
                            s_pe.done(last)
                        for n, p in images(slot, par, s, AT["s"][part] + 3):
                            b = (p + part) % 2
                            p_exp.wait(pe, n, part + 1)
                            if part >= 1:
                                pt_sb.wait(pe, n, part)
                            else:
                                pt_sb.wait(pe, n - 1, 3)
                            for row in range((g1 - g0) // 4):
                                last = tr(pt_ps[:, 128 * row:128 * row + 128],
                                          probs[:, b, row, :, :].rearrange("p t k -> p (t k)"), ident[:, :])
                            pt_pe.done(last)
                        for n, p in images(slot, par, s, AT["s"][part] + 5):
                            b = (p + part) % 2
                            pt_sb.wait(pe, n, part + 1)
                            if part >= 1:
                                o_sb.wait(pe, n, part)
                            else:
                                o_sb.wait(pe, n - 1, 3)
                            for g in range(g0, g1):
                                row, j = (g - g0) // 4, g % 4
                                last = mm(o_ps[32 * j:32 * j + 32, 128 * row:128 * row + 128], probsT[:, b, row, 32 * j:32 * j + 32],
                                          kvb[:, g, :, HD:2 * HD], start=True, stop=True)
                            av_pe.done(last)
                    for job, (w0, w1) in enumerate(XCUT):
                        for n, p in images(slot, par, s, AT["x"][job]):
                            x_cols.wait(pe, n, job + 1)
                            turn(F_READ, n, F_X + job)
                            for w in range(w0, w1):
                                last = tr(f_ps[(p + F_X + job) % 2][:, XROWS * (w - w0):XROWS * (w - w0) + XROWS],
                                          xcols[:, 128 * w:128 * w + 128], ident[0:XROWS, 0:XROWS])
                            x_tr.done(last)
                    for m in range(2):
                        for n, p in images(slot, par, s, AT["tok"][m]):
                            x_lo.wait(pe, n, 3)
                            turn(F_READ, n, F_TOK + m)
                            terms = [(a, b, ch) for ch in range(KCH) for a, b in ((0, 0), (0, 1), (1, 0))]
                            for t, (a, b, ch) in enumerate(terms):
                                last = mm(f_ps[(p + F_TOK + m) % 2][:, 0:PATCHES], wtok[:, a, ch, 128 * m:128 * m + 128],
                                          xT[:, b, GRID * ch:GRID * ch + GRID, :], start=t == 0, stop=t == len(terms) - 1)
                            tok_pe.done(last)
                    for n, p in images(slot, par, s, AT["stat"]):
                        turn(F_READ, n, F_STAT)
                        sums_pool.wait(pe, n, 8)
                        for c in range(TILES):
                            rows = TT if c < 2 else LASTP
                            for v in range(2):
                                last = mm(f_ps[(p + F_STAT) % 2][0:rows, 2 * c + v:2 * c + v + 1],
                                          xspread[:, v, :, :].rearrange("p i w -> p (i w)")[:, TT * c:TT * c + rows],
                                          ones[0:XROWS, 0:1], start=True, stop=True)
                        stat_pe.done(last)
                    for c in range(TILES):
                        rows = TT if c < 2 else LASTP
                        for n, p in images(slot, par, s, AT["y"][c]):
                            yT_sb.wait(pe, n, 2)
                            turn(F_READ, n, F_Y + c)
                            for m in range(2):
                                last = tr(f_ps[(p + F_Y + c) % 2][0:rows, 128 * m:128 * m + 128], yT[:, m, TT * c:TT * c + rows], ident[:, :])
                            y_pe.done(last)
                    for k in range(2):
                        for n, p in images(slot, par, s, AT["xt"][k]):
                            xn_sb.wait(pe, n, 3)
                            turn(F_READ, n, F_XT + k)
                            for c in range(TILES):
                                last = tr(f_ps[(p + F_XT + k) % 2][:, TT * c:TT * c + TT], yxn[:, c, 128 * k:128 * k + 128], ident[0:TT, 0:TT])
                            xn_pe.done(last)
                    for job in range(6):
                        for n, p in images(slot, par, s, AT["qkv"][job]):
                            c, half = job // 2, job % 2
                            xn_lo.wait(pe, n, 2)
                            turn(F_READ, n, F_QKV + job)
                            qkv_pe.done(product(f_ps[(p + F_QKV + job) % 2][0:TT, 0:NQ], lambda a, k: xnT[:, a, k, TT * c:TT * c + TT],
                                                lambda b, k: wqkv[:, b, k, NQ * half:NQ * half + NQ]))
                    for k in range(2):
                        for n, p in images(slot, par, s, AT["ont"][k]):
                            on_in.wait(pe, n, 1)
                            turn(T_READ, n, T_ON + k)
                            for c in range(TILES):
                                last = tr(t_ps[(p + T_ON + k) % 2][:, TT * c:TT * c + TT], on[:, c, 128 * k:128 * k + 128], ident[0:TT, 0:TT])
                            on_pe.done(last)
                    for c in range(TILES):
                        for n, p in images(slot, par, s, AT["wo"][c]):
                            on_lo.wait(pe, n, 2)
                            turn(T_READ, n, T_WO + c)
                            wo_pe.done(product(t_ps[(p + T_WO + c) % 2][0:TT, 0:E], lambda a, k: onT[:, a, k, TT * c:TT * c + TT],
                                               lambda b, k: wmat["woT"][:, b, k, :]))
                    for k in range(2):
                        for n, p in images(slot, par, s, AT["zt"][k]):
                            z_sb.wait(pe, n, 3)
                            turn(T_READ, n, T_ZT + k)
                            for c in range(TILES):
                                last = tr(t_ps[(p + T_ZT + k) % 2][:, TT * c:TT * c + TT], z[:, c, 128 * k:128 * k + 128], ident[0:TT, 0:TT])
                            z_pe.done(last)
                    for m in range(2):
                        for n, p in images(slot, par, s, AT["k"][m]):
                            mix_lo.wait(pe, n, 2)
                            turn(T_READ, n, T_K + m)
                            k_pe.done(product(t_ps[(p + T_K + m) % 2][:, 0:TP], lambda a, k: wmat["wkfT"][:, a, k, 128 * m:128 * m + 128],
                                              lambda b, k: mixp[:, 0, b, k, :]))
                    for c in range(TILES):
                        for n, p in images(slot, par, s, AT["r"][c]):
                            mix_lo.wait(pe, n, 4)
                            turn(T_READ, n, T_R + c)
                            r_pe.done(product(t_ps[(p + T_R + c) % 2][0:TT, 0:E], lambda a, k: mixp[:, 1, a, k, TT * c:TT * c + TT],
                                              lambda b, k: wmat["wrT"][:, b, k, :]))
                        for n, p in images(slot, par, s, AT["val"][c]):
                            ka_lo.wait(pe, n, 2)
                            turn(T_READ, n, T_VAL + c)
                            val_pe.done(product(t_ps[(p + T_VAL + c) % 2][0:TT, 0:E], lambda a, k: kaT[:, a, k, TT * c:TT * c + TT],
                                                lambda b, k: wmat["wvfT"][:, b, k, :]))

            slots(pe, body)


INPUTS = ["x", "txt", "L0_tok_ln1_g", "L0_tok_ln1_b", "L0_tok_W", "L0_tok_b", "L0_tok_ln2_g", "L0_tok_ln2_b",
          "L0_attn_Wq", "L0_attn_bq", "L0_attn_Wk", "L0_attn_bk", "L0_attn_Wv", "L0_attn_bv", "L0_attn_Wo",
          "L0_attn_bo", "L0_ffn_W_r", "L0_ffn_W_k", "L0_ffn_W_v", "L0_ffn_mu_r", "L0_ffn_mu_k"]


def kernel(**inputs):
    import numpy as np
    import concourse.bacc as bacc
    from concourse.bass_utils import run_bass_kernel_spmd

    nc = bacc.Bacc("TRN2", target_bir_lowering=False, num_devices=1)
    arrays, args = {}, []
    for name in INPUTS:
        a = np.ascontiguousarray(inputs[name])
        arrays[f"in_{name}"] = a
        args.append(nc.dram_tensor(f"in_{name}", a.shape, mybir.dt.from_np(a.dtype), kind="ExternalInput").ap())
    args.append(nc.dram_tensor("out", (IMAGES, T, E), F32, kind="ExternalOutput").ap())
    fusion_kernel(nc, *args)
    return run_bass_kernel_spmd(nc, [arrays], core_ids=[0]).results[0]["out"]
```

```python
from contextlib import ExitStack

import concourse.bass as bass
from concourse import mybir

F32 = mybir.dt.float32
F32R = mybir.dt.float32r
ALU = mybir.AluOpType
ACT = mybir.ActivationFunctionType
AX = mybir.AxisListType

IMAGES, CH, SIDE = 64, 3, 224
PS = 16
GRID = SIDE // PS
PATCHES = GRID * GRID
HALF = PS // 2
XROWS = 2 * CH * GRID
KCH = 2 * CH
PDIM = KCH * 128
TXT = 77
T = PATCHES + TXT
TP = T + 1
E = 256
HEADS, HD = 16, 16
TT = 91
TILES = T // TT
LASTP = PATCHES - 2 * TT

GT = 8
GROUPS = 36
TG = GT * GROUPS
ROWS = GROUPS // 4
PARTS = [(0, 12), (12, 24), (24, 36)]
OUTS = 4 + 3
AVW = GT * (HD + 1)
QKV = 3 * HD
NQ = HEADS * QKV // 2
EPS = 1e-5

SLOT = 82
AT = dict(
    load=349, xcols=[365, 409, 424], stats=[367, 368, 369, 370, 398, 412, 420], sums=439, x=[408, 423, 428],
    xh=[410, 428, 438], xl=[425, 434, 442], tok=[443, 445], yt=[448, 450], stat=444, statc=444, rstd1=452,
    txt=461, y=[452, 453, 454], yn=[453, 455, 456], st2=[454, 457, 458], mv2=460, rstd2=462, hg=[462, 463, 468],
    h=[466, 470, 471], st3=[469, 472, 473], mv3=475, rstd3=478, xn=[482, 483, 485], xt=[486, 487], xnh=[488, 489],
    xnl=[489, 490], hb=535, qkv=[492, 497, 499, 502, 503, 504], qb=[497, 498, 500, 505, 508, 509], qkv_out=[502,
    506, 514], qkv_in=[515, 519, 520], spread=[531, 533, 534, 540, 548, 550, 551, 552], s=[564, 567, 570],
    mx=[567, 574, 581], sub=[570, 577, 583], exp=[572, 583, 586], pt=[580, 588, 591], ptc=[587, 594, 600],
    av=[595, 599, 600], rec=[599, 601, 605], osb=[600, 604, 607], o_out=610, o_in=614, ont=[621, 622], onh=[623,
    625], onl=[628, 629], wo=[631, 639, 640], h2=[638, 643, 646], st4=[645, 647, 648], mv4=650, rstd4=655, z=[657,
    658, 662], zt=[664, 665], ztc=[666, 667], d=[669, 673], mix=[670, 676, 677, 679], mixh=[675, 677, 678, 690],
    mixl=[682, 683, 684, 694], k=[685, 686], kr=[691, 692], ksq=[697, 703], kah=[702, 709], kal=[705, 715],
    r=[702, 706, 724], rt=[706, 713, 725], val=[716, 723, 726], rv=[724, 739, 742], add=[736, 739, 777], out=[746,
    750, 790])
BANK = dict(
    x=[3, 0, 1], tok=[1, 3], stat=[4], y=[7, 4, 7], xt=[6, 2], qkv=[7, 1, 2, 7, 2, 5], s=[3, 4, 0], pt=[6, 7, 4],
    av=[3, 6, 7], ont=[2, 1], wo=[5, 4, 2], zt=[4, 1], k=[5, 2], r=[4, 4, 7], val=[0, 1, 5])

XCUT = [(0, 5), (5, 10), (10, 14)]


def images(slot, slot_parity, step, offset):
    if (step - offset) % SLOT == 0:
        back = (step - offset) // SLOT
        n = slot + back
        if not isinstance(slot, int) or 0 <= n < IMAGES:
            yield n, (slot_parity + back) % 2


class Signal:

    def __init__(self, ctx, nc, name, per, primed=False, unit=1):
        self.sem = ctx.enter_context(nc.semaphore(name))
        self.per, self.unit = per * unit, unit
        self.base = 2 * self.per if primed else 0

    def wait(self, eng, n, count):
        eng.wait_ge(self.sem, n * self.per + (self.base + count * self.unit))

    def done(self, ins):
        ins.then_inc(self.sem, self.unit)
        return ins


def fusion_kernel(nc, x, txt, ln1_g, ln1_b, tok_w, tok_b, ln2_g, ln2_b, wq, bq, wk, bk, wv, bv, wo, bo,
                  w_r, w_k, w_v, mu_r, mu_k, out):
    with ExitStack() as ctx:
        def sb(name, shape, dt=F32):
            return ctx.enter_context(nc.sbuf_tensor(name, shape, dt))

        def sig(name, per, primed=False, unit=1):
            return Signal(ctx, nc, name, per, primed, unit)

        ident = sb("ident", [128, 128])
        ones = sb("ones", [128, 128])
        rowmask = sb("rowmask", [XROWS, GRID])
        tokmask = sb("tokmask", [128, GT])
        g2b, b2b, c0b, bob = (sb(n, [128, E]) for n in ("g2b", "b2b", "c0b", "bob"))
        bqkv = sb("bqkv", [128, HEADS, QKV])
        mus = sb("mus", [128, 2, 2])
        small = sb("small", [128, 16])
        epst, minus, powt = (small[:, k:k + TILES] for k in (0, 4, 8))
        wtok = sb("wtok", [128, 2, KCH, E], F32R)
        wqkv = sb("wqkv", [128, 2, 2, HEADS * QKV], F32R)
        wmat = {n: sb(n, [128, 2, 2, E], F32R) for n in ("woT", "wrT", "wkfT", "wvfT")}

        xim = sb("xim", [XROWS, HALF * SIDE])
        xcols = sb("xcols", [XROWS, GRID * 128])
        xst = sb("xst", [XROWS, GRID, 6])
        xs = sb("xs", [XROWS, 2, GRID])
        xtmp = sb("xtmp", [XROWS, 2, GRID])
        xspread = sb("xspread", [XROWS, 2, GRID, GRID])
        xT = sb("xT", [128, 2, KCH * GRID, GRID], F32R)
        stat1 = sb("stat1", [TT, TILES, 2])
        var1 = sb("var1", [TT, 2, TILES])
        rstd1 = sb("rstd1", [TT, TILES])
        yT = sb("yT", [128, 2, PATCHES])
        bn2, bn3, bn4 = (sb(n, [TT, TILES, 6]) for n in ("bn2", "bn3", "bn4"))
        mv2, mv3, mv4 = (sb(n, [TT, TILES, 2]) for n in ("mv2", "mv3", "mv4"))
        ve2, ve3, ve4 = (sb(n, [TT, TILES]) for n in ("ve2", "ve3", "ve4"))
        rs2, rs3, rs4 = (sb(n, [TT, TILES]) for n in ("rs2", "rs3", "rs4"))
        nm3, nm4 = (sb(n, [TT, TILES]) for n in ("nm3", "nm4"))
        yxn = sb("yxn", [TT, TILES, E])
        h = sb("h", [TT, TILES, E])
        hb = sb("hb", [TT, 2, TILES, E])
        xnT = sb("xnT", [128, 2, 2, TP], F32R)
        qkvt = sb("qkvt", [TT, TILES, HEADS * QKV])

        qkv = sb("qkv", [128, GROUPS, QKV])
        kvb = sb("kvb", [128, GROUPS, GT, 2 * HD + 1])
        probs = sb("probs", [128, ROWS, GT, HD])
        mx = sb("mx", [128, ROWS * GT])
        rsum = sb("rsum", [128, ROWS * GT])
        probsT = sb("probsT", [128, ROWS, 128])
        osb = sb("osb", [128, ROWS, 128])

        on = sb("on", [TT, TILES, E])
        onT = sb("onT", [128, 2, 2, TP], F32R)
        h2 = sb("h2", [TT, 2, TILES, E])
        z = sb("z", [TT, TILES, E])
        zT = sb("zT", [128, 2, TP])
        dT = sb("dT", [128, 2, TP])
        mixf = sb("mixf", [128, 4, TP])
        mixp = sb("mixp", [128, 2, 2, 2, TP], F32R)
        kr = sb("kr", [128, 2, TP])
        kaf = sb("kaf", [128, 2, TP])
        kaT = sb("kaT", [128, 2, 2, TP], F32R)
        r = sb("r", [TT, TILES, E])
        rv = sb("rv", [TT, TILES, E])

        def bank(name):
            return ctx.enter_context(nc.psum_tensor(name, [128, 512], F32))

        banks = [bank(f"bank{i}") for i in range(8)]

        qkv_dram = nc.dram_tensor("qkv_dram", (TG, HEADS, QKV), F32, kind="Internal").ap()
        o_dram = nc.dram_tensor("o_dram", (HEADS, T, HD), F32, kind="Internal").ap()

        raw_in = ctx.enter_context(nc.semaphore("raw_in"))
        prep_pe = ctx.enter_context(nc.semaphore("prep_pe"))
        prep_dve = ctx.enter_context(nc.semaphore("prep_dve"))
        prep_pool = ctx.enter_context(nc.semaphore("prep_pool"))
        ready = ctx.enter_context(nc.semaphore("ready"))
        settled = ctx.enter_context(nc.semaphore("settled"))

        def settle(eng):
            eng.sem_inc(settled, 1)

        x_in = sig("x_in", 2, unit=16)
        txt_in = sig("txt_in", 1, unit=16)
        x_stats = sig("x_stats", 1, True)
        sums_pool = sig("sums_pool", 8, True)
        x_cols = sig("x_cols", 3, True)
        x_tr = sig("x_tr", 3, True)
        x_hi = sig("x_hi", 3)
        x_lo = sig("x_lo", 3)
        stat_pe = sig("stat_pe", 1, True)
        stat_sb = sig("stat_sb", 2)
        rstd1_pool = sig("rstd1_pool", 5, True)
        tok_pe = sig("tok_pe", 2, True)
        yT_sb = sig("yT_sb", 2)
        y_pe = sig("y_pe", 3, True)
        y_sb = sig("y_sb", 3, True)
        st2 = sig("st2", 3)
        mv2_sb = sig("mv2_sb", 3)
        rs2_pool = sig("rs2_pool", 2, True)
        hg = sig("hg", 3)
        h_sb = sig("h_sb", 3, True)
        st3 = sig("st3", 3)
        mv3_sb = sig("mv3_sb", 3)
        rs3_pool = sig("rs3_pool", 4)
        xn_sb = sig("xn_sb", 3, True)
        xn_pe = sig("xn_pe", 2, True)
        xn_hi = sig("xn_hi", 2)
        xn_lo = sig("xn_lo", 2)
        qkv_pe = sig("qkv_pe", 6, True)
        qkv_sb = sig("qkv_sb", 6, True)
        qkv_out = [sig(f"qkv_out{c}", 1, True, unit=16) for c in range(TILES)]
        qkv_in = sig("qkv_in", 3, True, unit=16)
        hb_sb = sig("hb_sb", 1, True)
        kvb_sb = sig("kvb_sb", 8, True)
        s_pe = sig("s_pe", 3, True)
        mx_sb = sig("mx_sb", 3)
        s_sub = sig("s_sub", 3, True)
        p_exp = sig("p_exp", 3)
        rsum_sb = sig("rsum_sb", 3)
        pt_pe = sig("pt_pe", 3, True)
        pt_sb = sig("pt_sb", 3, True)
        av_pe = sig("av_pe", 3, True)
        o_sb = sig("o_sb", 3, True)
        o_out = sig("o_out", OUTS, True, unit=16)
        on_in = sig("on_in", 1, True, unit=16)
        on_pe = sig("on_pe", 2, True)
        on_hi = sig("on_hi", 2)
        on_lo = sig("on_lo", 2)
        wo_pe = sig("wo_pe", 3, True)
        h2_sb = sig("h2_sb", 3, True)
        st4 = sig("st4", 3)
        mv4_sb = sig("mv4_sb", 3)
        rs4_pool = sig("rs4_pool", 4, True)
        z_sb = sig("z_sb", 3, True)
        z_pe = sig("z_pe", 2, True)
        zT_sb = sig("zT_sb", 2)
        d_sb = sig("d_sb", 2)
        mix_sb = sig("mix_sb", 4, True)
        mix_hi = sig("mix_hi", 4)
        mix_lo = sig("mix_lo", 4, True)
        k_pe = sig("k_pe", 2, True)
        kr_sb = sig("kr_sb", 2)
        ka_sb = sig("ka_sb", 2, True)
        ka_hi = sig("ka_hi", 2)
        ka_lo = sig("ka_lo", 2, True)
        r_pe = sig("r_pe", 3, True)
        r_tanh = sig("r_tanh", 3)
        val_pe = sig("val_pe", 3, True)
        rv_sb = sig("rv_sb", 3, True)
        out_sb = sig("out_sb", 3, True)
        out_dma = sig("out_dma", 3, True, unit=16)
        primed = [s for s in locals().values() if isinstance(s, Signal) and s.base] + qkv_out

        READ = dict(x=x_lo, tok=yT_sb, stat=stat_sb, y=y_sb, xt=xn_lo, qkv=qkv_sb, s=s_sub, pt=pt_sb, av=o_sb,
                    ont=on_lo, wo=h2_sb, zt=zT_sb, k=kr_sb, r=r_tanh, val=rv_sb)

        def step_of(kind, j):
            return AT[kind][j] if isinstance(AT[kind], list) else AT[kind]

        JOBS = sorted(((kind, j) for kind in BANK for j in range(len(BANK[kind]))), key=lambda job: step_of(*job) % SLOT)

        def place(kind, j):
            return banks[BANK[kind][j]]

        block = ctx.enter_context(nc.Block())

        offsets = [o for at in AT.values() for o in (at if isinstance(at, list) else [at])]
        FIRST = max(offsets) // SLOT + 1
        LAST = IMAGES + min(offsets) // SLOT
        LAST -= (LAST - FIRST) % 2
        END = IMAGES + max(offsets) // SLOT

        def slots(eng, body):
            for slot in range(min(offsets) // SLOT, FIRST):
                body(slot, slot % 2)
            with eng.Fori(0, (LAST - FIRST) // 2) as i:
                for u in range(2):
                    body(i * 2 + (FIRST + u), (FIRST + u) % 2)
            for slot in range(LAST, END):
                body(slot, slot % 2)

        flat = kvb[:, :, :, :].rearrange("p g t c -> p (g t c)")
        raw = flat[:, 0:PDIM // 128 * E].rearrange("p (c e) -> p c e", c=KCH)
        c0rep = flat[:, 1536:1536 + PDIM].rearrange("p (c m) -> p c m", c=KCH)
        bnat = flat[:, 2304:2304 + 3 * E].rearrange("p (x e) -> p x e", x=3)
        lnt = flat[:, 3072:3084]
        WEIGHTS = [wq, wk, wv, wo, w_r, w_k, w_v]
        rawsq = flat[:, 3584:3584 + 7 * 2 * E].rearrange("p (n a e) -> p n a e", n=7, a=2)
        DVE_TOK = KCH + 1 + KCH + 1 + KCH + 2
        RAWS = 4 + 2 + 7 + 2 + 7 + 1

        @block.sync
        def _(sp):
            with nc.allow_non_contiguous_dma(reason="small vectors, once"):
                for c in range(2):
                    sp.dma_start(lnt[:, 3 * c:3 * c + 3], ln1_g[384 * c:384 * c + 384].rearrange("(p c) -> p c", c=CH)).then_inc(raw_in, 16)
                    sp.dma_start(lnt[:, 6 + 3 * c:9 + 3 * c], ln1_b[384 * c:384 * c + 384].rearrange("(p c) -> p c", c=CH)).then_inc(raw_in, 16)
                for s, v in ((0, mu_k), (1, mu_r)):
                    sp.dma_start(mus[:, s, :], v.rearrange("(k p) -> p k", p=128)).then_inc(raw_in, 16)
                for dst, v in ((g2b[:, :], ln2_g), (b2b[:, :], ln2_b), (c0b[:, :], tok_b), (bob[:, :], bo),
                               (bnat[:, 0, :], bq), (bnat[:, 1, :], bk), (bnat[:, 2, :], bv)):
                    sp.dma_start(dst, v.rearrange("(a e) -> a e", a=1).broadcast_to((128, E))).then_inc(raw_in, 16)
            for half in range(2):
                sp.dma_start(raw[:, 3 * half:3 * half + 3, :],
                             tok_w[384 * half:384 * half + 384, :].rearrange("(p c) e -> p c e", c=CH)).then_inc(raw_in, 16)
            for n, w in enumerate(WEIGHTS):
                sp.dma_start(rawsq[:, n, :, :], w.rearrange("(a p) e -> p a e", p=128)).then_inc(raw_in, 16)
            sp.wait_ge(prep_pool, 1)
            sp.dma_start(qkv_dram[T:TG, :, :].rearrange("t i j -> t (i j)"), qkvt[0:TG - T, 0, :]).then_inc(raw_in, 16)

            def after(signal, n, count):
                signal.wait(sp, n, count)
                settle(sp)

            def body(slot, par):
                for s in range(SLOT):
                    for n, p in images(slot, par, s, AT["load"]):
                        after(x_cols, n - 1, 3)
                        after(x_stats, n - 1, 1)
                        for half in range(2):
                            src = x[bass.ds(n, 1), :, :, :].rearrange("b c (i r) w -> (b c i) (r w)", r=PS)
                            x_in.done(sp.dma_start(xim[half * 42:half * 42 + 42, :],
                                                   src[:, half * HALF * SIDE:(half + 1) * HALF * SIDE]))
                    for n, p in images(slot, par, s, AT["txt"]):
                        after(hb_sb, n - 1, 1)
                        after(xn_sb, n - 1, 3)
                        txt_in.done(sp.dma_start(h[LASTP:TT, 2, :], txt[bass.ds(n, 1), :, :].rearrange("b t e -> (b t) e")))
                    for c in range(TILES):
                        for n, p in images(slot, par, s, AT["qkv_out"][c]):
                            after(qkv_sb, n, 2 * c + 2)
                            if c == 0:
                                after(qkv_in, n - 1, 3)
                            qkv_out[c].done(sp.dma_start(qkv_dram[TT * c:TT * c + TT, :, :].rearrange("t i j -> t (i j)"), qkvt[:, c, :]))
                    for c in range(TILES):
                        for n, p in images(slot, par, s, AT["qkv_in"][c]):
                            g0, g1 = TT * c // GT, TT * (c + 1) // GT if c < 2 else GROUPS
                            after(qkv_out[c], n, 1)
                            if c == 0:
                                after(kvb_sb, n - 1, 8)
                                after(s_pe, n - 1, 3)
                            qkv_in.done(sp.dma_start(qkv[:, g0:g1, :], qkv_dram[GT * g0:GT * g1, :, :].rearrange("(g t) i j -> (t i) g j", t=GT)))
                    for n, p in images(slot, par, s, AT["o_out"]):
                        after(o_sb, n, 3)
                        after(on_in, n - 1, 1)
                        full = T // (4 * GT)
                        dst = o_dram[:, 0:4 * GT * full, :].rearrange("q (b j t) d -> q j b (t d)", b=full, j=4)
                        for j in range(4):
                            o_out.done(sp.dma_start(dst[:, j, :, :], osb[32 * j:32 * j + HEADS, 0:full, :]))
                        for j in range(OUTS - 4):
                            t0 = GT * (4 * full + j)
                            t1 = min(t0 + GT, T)
                            o_out.done(sp.dma_start(o_dram[:, t0:t1, :].rearrange("q t d -> q (t d)"),
                                                    osb[32 * j:32 * j + HEADS, full, 0:HD * (t1 - t0)]))
                    for n, p in images(slot, par, s, AT["o_in"]):
                        after(o_out, n, OUTS)
                        after(on_pe, n - 1, 2)
                        rows = o_dram.rearrange("q t d -> (q t d)").rearrange("(c p e) -> p c e", c=TILES, e=E)
                        on_in.done(sp.dma_start(on[:, :, :], rows))
                    for c in range(TILES):
                        for n, p in images(slot, par, s, AT["out"][c]):
                            after(out_sb, n, c + 1)
                            if c == 0:
                                after(out_dma, n - 1, 3)
                            o = out[bass.ds(n, 1), :, :].rearrange("b t e -> (b t) e")
                            out_dma.done(sp.dma_start(o[TT * c:TT * c + TT, :], h2[:, p, c, :]))

            slots(sp, body)
            out_dma.wait(sp, IMAGES - 1, 3)
            qkv_in.wait(sp, IMAGES - 1, 3)
            on_in.wait(sp, IMAGES - 1, 1)

        @block.gpsimd
        def _(pool):
            def prep(ins):
                ins.then_inc(prep_pool, 1)

            prep(nc.gpsimd.memset(qkvt[0:TG - T, 0, :], 0.0))
            prep(nc.gpsimd.memset(ident[:, :], 0.0))
            prep(nc.gpsimd.memset(tokmask[:, :], 1.0))
            prep(nc.gpsimd.memset(ones[:, :], 1.0))
            pool.wait_ge(prep_pool, 4)
            prep(nc.gpsimd.affine_select(out=ident[:, :], in_=ident[:, :], compare_op=ALU.not_equal, fill=1.0,
                                         base=0, pattern=[[-1, 128]], channel_multiplier=1))
            prep(nc.gpsimd.affine_select(out=tokmask[:, :], in_=tokmask[:, :], compare_op=ALU.is_ge, fill=0.0,
                                         base=0, pattern=[[-HD, GT]], channel_multiplier=1))
            pool.wait_ge(prep_pool, 6)
            prep(nc.gpsimd.affine_select(out=tokmask[:, :], in_=tokmask[:, :], compare_op=ALU.is_ge, fill=0.0,
                                         base=HD - 1, pattern=[[HD, GT]], channel_multiplier=-1))
            for k in range(KCH):
                src = ident[0:XROWS, GRID * k:GRID * k + GRID]
                if k == 0:
                    prep(nc.gpsimd.tensor_copy(rowmask[:, :], src))
                else:
                    prep(nc.gpsimd.tensor_tensor(rowmask[:, :], rowmask[:, :], src, ALU.add))
                pool.wait_ge(prep_pool, 8 + k)
            prep(nc.gpsimd.memset(small[:, 0:4], EPS))
            prep(nc.gpsimd.memset(small[:, 4:8], -1.0))
            prep(nc.gpsimd.memset(small[:, 8:16], -0.5))
            zeroed = (stat1, mv2, zT, dT, mixf, kr)
            for t in zeroed:
                prep(nc.gpsimd.memset(t[:], 0.0))
            pool.wait_ge(prep_pool, 16 + len(zeroed))
            for s in primed:
                pool.sem_inc(s.sem, s.base)
            pool.wait_ge(ready, 1)

            def rsqrt(n, mv, ve, rs, done, nm=None):
                done.done(nc.gpsimd.tensor_tensor(ve[:, :], mv[:, :, 1], epst[0:TT, :], ALU.add))
                done.wait(pool, n, 1)
                done.done(nc.gpsimd.tensor_tensor(rs[:, :], ve[:, :], powt[0:TT, :], ALU.pow))
                if nm is not None:
                    done.done(nc.gpsimd.tensor_tensor(nm[:, :], mv[:, :, 0], minus[0:TT, :], ALU.mult))
                    done.wait(pool, n, 3)
                    done.done(nc.gpsimd.tensor_tensor(nm[:, :], nm[:, :], rs[:, :], ALU.mult))

            def body(slot, par):
                for s in range(SLOT):
                    for n, p in images(slot, par, s, AT["sums"]):
                        me, mo, ve, vo = (xst[:, :, k] for k in (1, 4, 2, 5))
                        x_stats.wait(pool, n, 1)
                        stat_pe.wait(pool, n - 1, 1)
                        sums_pool.done(nc.gpsimd.tensor_tensor(xs[:, 0, :], me, mo, ALU.add))
                        sums_pool.done(nc.gpsimd.tensor_tensor(xs[:, 1, :], me, me, ALU.mult))
                        sums_pool.done(nc.gpsimd.tensor_tensor(xtmp[:, 0, :], mo, mo, ALU.mult))
                        sums_pool.done(nc.gpsimd.tensor_tensor(xtmp[:, 1, :], ve, vo, ALU.add))
                        sums_pool.wait(pool, n, 4)
                        sums_pool.done(nc.gpsimd.tensor_tensor(xs[:, 1, :], xs[:, 1, :], xtmp[:, 0, :], ALU.add))
                        sums_pool.done(nc.gpsimd.tensor_scalar(xtmp[:, 1, :], xtmp[:, 1, :], 2.0 / (HALF * PS), None, ALU.mult))
                        sums_pool.wait(pool, n, 6)
                        sums_pool.done(nc.gpsimd.tensor_tensor(xs[:, 1, :], xs[:, 1, :], xtmp[:, 1, :], ALU.add))
                        sums_pool.wait(pool, n, 7)
                        sums_pool.done(nc.gpsimd.tensor_tensor(
                            xspread[:, :, :, :].rearrange("p s i w -> p i s w"),
                            xs[:, :, :].unsqueeze(1).broadcast_to((XROWS, GRID, 2, GRID)),
                            rowmask[:, :].unsqueeze(2).unsqueeze(3).broadcast_to((XROWS, GRID, 2, GRID)), ALU.mult))
                    for n, p in images(slot, par, s, AT["rstd1"]):
                        stat_sb.wait(pool, n, 2)
                        y_sb.wait(pool, n - 1, 3)
                        settle(pool)
                        rstd1_pool.done(nc.gpsimd.tensor_scalar(var1[:, :, :].rearrange("p s c -> p c s"), stat1[:, :, :],
                                                                1.0 / (2 * KCH), None, ALU.mult))
                        rstd1_pool.wait(pool, n, 1)
                        rstd1_pool.done(nc.gpsimd.tensor_tensor(var1[:, 0, :], var1[:, 0, :], var1[:, 0, :], ALU.mult))
                        rstd1_pool.wait(pool, n, 2)
                        rstd1_pool.done(nc.gpsimd.tensor_tensor(var1[:, 1, :], var1[:, 1, :], var1[:, 0, :], ALU.subtract))
                        rstd1_pool.wait(pool, n, 3)
                        rstd1_pool.done(nc.gpsimd.tensor_tensor(var1[:, 0, :], var1[:, 1, :], epst[0:TT, :], ALU.add))
                        rstd1_pool.wait(pool, n, 4)
                        rstd1_pool.done(nc.gpsimd.tensor_tensor(rstd1[:, :], var1[:, 0, :], powt[0:TT, :], ALU.pow))
                    for n, p in images(slot, par, s, AT["rstd2"]):
                        mv2_sb.wait(pool, n, 3)
                        h_sb.wait(pool, n - 1, 3)
                        rsqrt(n, mv2, ve2, rs2, rs2_pool)
                    for n, p in images(slot, par, s, AT["rstd3"]):
                        mv3_sb.wait(pool, n, 3)
                        xn_sb.wait(pool, n - 1, 3)
                        rsqrt(n, mv3, ve3, rs3, rs3_pool, nm3)
                    for n, p in images(slot, par, s, AT["hb"]):
                        h_sb.wait(pool, n, 3)
                        txt_in.wait(pool, n, 1)
                        h2_sb.wait(pool, n - 2, 3)
                        hb_sb.done(nc.gpsimd.tensor_tensor(hb[:, p, :, :], h[:, :, :],
                                                           bob[0:TT, :].unsqueeze(1).broadcast_to((TT, TILES, E)), ALU.add))
                    for n, p in images(slot, par, s, AT["rstd4"]):
                        mv4_sb.wait(pool, n, 3)
                        z_sb.wait(pool, n - 1, 3)
                        rsqrt(n, mv4, ve4, rs4, rs4_pool, nm4)
                    for k in range(2):
                        for n, p in images(slot, par, s, AT["d"][k]):
                            zT_sb.wait(pool, n, k + 1)
                            mix_sb.wait(pool, n - 1, 4)
                            d_sb.done(nc.gpsimd.tensor_tensor(dT[:, k, 0:T], zT[:, k, 1:TP], zT[:, k, 0:T], ALU.subtract))
                    for j in range(4):
                        for n, p in images(slot, par, s, AT["mixl"][j]):
                            w, k = j // 2, j % 2
                            mix_hi.wait(pool, n, j + 1)
                            (r_pe if w else k_pe).wait(pool, n - 1, 3 if w else 2)
                            mix_lo.done(nc.gpsimd.tensor_tensor(mixp[:, w, 1, k, :], mixf[:, j, :],
                                                                mixp[:, w, 0, k, :].bitcast(F32), ALU.subtract))
                    for m in range(2):
                        for n, p in images(slot, par, s, AT["ksq"][m]):
                            kr_sb.wait(pool, n, m + 1)
                            ka_lo.wait(pool, n - 1, 2)
                            ka_sb.done(nc.gpsimd.tensor_tensor(kaf[:, m, :], kr[:, m, :], kr[:, m, :], ALU.mult))
                        for n, p in images(slot, par, s, AT["kal"][m]):
                            ka_hi.wait(pool, n, m + 1)
                            val_pe.wait(pool, n - 1, 3)
                            ka_lo.done(nc.gpsimd.tensor_tensor(kaT[:, 1, m, :], kaf[:, m, :],
                                                               kaT[:, 0, m, :].bitcast(F32), ALU.subtract))
                    for c in range(TILES):
                        for n, p in images(slot, par, s, AT["add"][c]):
                            rv_sb.wait(pool, n, c + 1)
                            out_sb.done(nc.gpsimd.tensor_tensor(h2[:, p, c, :], h2[:, p, c, :], rv[:, c, :], ALU.add))

            slots(pool, body)

        @block.vector
        def _(dve):
            V = nc.vector
            count = [0]

            def prep(ins):
                ins.then_inc(prep_dve, 1)
                count[0] += 1
                return count[0]

            dve.wait_ge(raw_in, RAWS * 16)
            dve.wait_ge(prep_pool, 6)
            wsum = yT[:, :, :].rearrange("p m t -> p (m t)")[:, 0:E]
            for ch in range(KCH):
                prep(V.tensor_scalar(c0rep[:, ch, :], ones[:, :], lnt[:, 6 + ch:7 + ch], None, ALU.mult))
            dve.wait_ge(prep_pe, 1)
            c = prep(V.tensor_tensor(c0b[:, :], banks[0][:, 0:E], c0b[:, :], ALU.add))
            for ch in range(KCH):
                c = prep(V.tensor_scalar(raw[:, ch, :], raw[:, ch, :], lnt[:, ch:ch + 1], None, ALU.mult))
            dve.wait_ge(prep_pe, 2)
            c = prep(V.tensor_scalar(wsum, banks[2][:, 0:E], 1.0 / PDIM, None, ALU.mult))
            dve.wait_ge(prep_dve, c)
            for ch in range(KCH):
                c = prep(V.tensor_tensor(raw[:, ch, :], raw[:, ch, :], wsum, ALU.subtract))
            dve.wait_ge(prep_dve, c)
            c = prep(V.tensor_copy(wtok[:, 0, :, :], raw))
            dve.wait_ge(prep_dve, c)
            c = prep(V.tensor_tensor(wtok[:, 1, :, :], raw, wtok[:, 0, :, :].bitcast(F32), ALU.subtract))
            assert c == DVE_TOK
            for n in range(len(WEIGHTS)):
                scale = {0: HD ** -0.5, 6: 0.5}.get(n, 1.0)
                dve.wait_ge(prep_pe, 3 + n)
                for k in range(2):
                    src = banks[n % 2][:, E * k:E * k + E]
                    if n < 3:
                        src = src.rearrange("p (h d) -> p d h", d=HD) if n < 2 else src.rearrange("p (h d) -> p h d", d=HD)
                        hi, lo = (wqkv[:, a, k, :].rearrange("p (i c) -> p i c", c=QKV)[:, :, HD * n:HD * n + HD] for a in range(2))
                    else:
                        hi, lo = (wmat[("woT", "wrT", "wkfT", "wvfT")[n - 3]][:, a, k, :] for a in range(2))
                    c = prep(V.tensor_scalar(hi, src, scale, None, ALU.mult))
                    dve.wait_ge(prep_dve, c)
                    c = prep(V.scalar_tensor_tensor(out=lo, in0=src, scalar=scale, in1=hi.bitcast(F32),
                                                    op0=ALU.mult, op1=ALU.subtract))
            for n in range(3):
                src = bnat[:, n, :].rearrange("p (h d) -> p d h", d=HD) if n < 2 else bnat[:, n, :].rearrange("p (h d) -> p h d", d=HD)
                c = prep(V.tensor_scalar(bqkv[:, :, HD * n:HD * n + HD], src, HD ** -0.5 if n == 0 else 1.0, None, ALU.mult))
            dve.wait_ge(prep_dve, c)
            dve.wait_ge(prep_pool, 22)
            c = prep(V.tensor_copy(kvb[:, :, :, 2 * HD], tokmask[:, :].unsqueeze(1).broadcast_to((128, GROUPS, GT))))
            dve.wait_ge(prep_dve, c)
            dve.sem_inc(ready, 1)

            def aggregate(n, c, bn, st, mv, mv_sb, rows=TT):
                st.wait(dve, n, c + 1)
                settle(dve)
                mv_sb.done(V.bn_aggr(mv[0:rows, c, :], bn[0:rows, c, :]))

            def body(slot, par):
                for s in range(SLOT):
                    for part, (g0, g1) in enumerate(PARTS):
                        r0, r1 = g0 // 4, g1 // 4
                        for n, p in images(slot, par, s, AT["mx"][part]):
                            sc = place("s", part)[:, 0:128 * (r1 - r0)].rearrange("p (t k) -> p t k", k=HD)
                            s_pe.wait(dve, n, part + 1)
                            mx_sb.done(V.tensor_reduce(mx[:, GT * r0:GT * r1], sc, AX.X, ALU.max))
                        for n, p in images(slot, par, s, AT["sub"][part]):
                            sc = place("s", part)[:, 0:128 * (r1 - r0)].rearrange("p (t k) -> p t k", k=HD)
                            mx_sb.wait(dve, n, part + 1)
                            pt_pe.wait(dve, n - 1, part + 1)
                            s_sub.done(V.tensor_tensor(probs[:, r0:r1, :, :].rearrange("p b t k -> p (b t) k"), sc,
                                                       mx[:, GT * r0:GT * r1].unsqueeze(2).broadcast_to((128, GT * (r1 - r0), HD)), ALU.subtract))
                        val = place("av", part)[:, 0:GT * (r1 - r0) * (HD + 1)].rearrange("p (t d) -> p t d", d=HD + 1)
                        for n, p in images(slot, par, s, AT["rec"][part]):
                            av_pe.wait(dve, n, part + 1)
                            rsum_sb.done(V.reciprocal(rsum[:, GT * r0:GT * r1].unsqueeze(2), val[:, :, HD:HD + 1]))
                        for n, p in images(slot, par, s, AT["osb"][part]):
                            av_pe.wait(dve, n, part + 1)
                            rsum_sb.wait(dve, n, part + 1)
                            o_out.wait(dve, n - 1, OUTS)
                            o_sb.done(V.tensor_tensor(osb[:, r0:r1, :].rearrange("p b (t d) -> p (b t) d", d=HD),
                                                      val[:, :, 0:HD],
                                                      rsum[:, GT * r0:GT * r1].unsqueeze(2).broadcast_to((128, GT * (r1 - r0), HD)), ALU.mult))
                    for k in range(7):
                        for n, p in images(slot, par, s, AT["stats"][k]):
                            if k == 0:
                                x_in.wait(dve, n, 2)
                                sums_pool.wait(dve, n - 1, 4)
                            for w in (2 * k, 2 * k + 1):
                                last = V.bn_stats(xst[:, w, :], xim[:, :].rearrange("p (r w) -> p r w", w=SIDE)[:, :, PS * w:PS * w + PS])
                            if k == 6:
                                x_stats.done(last)
                    for job, (w0, w1) in enumerate(XCUT):
                        for n, p in images(slot, par, s, AT["xl"][job]):
                            x_hi.wait(dve, n, job + 1)
                            src = place("x", job)[:, 0:XROWS * (w1 - w0)].rearrange("p (w j) -> p j w", j=XROWS)
                            x_lo.done(V.tensor_tensor(xT[:, 1, :, w0:w1], src, xT[:, 0, :, w0:w1].bitcast(F32), ALU.subtract))
                    for n, p in images(slot, par, s, AT["statc"]):
                        stat_pe.wait(dve, n, 1)
                        rstd1_pool.wait(dve, n - 1, 5)
                        src = place("stat", 0)
                        stat_sb.done(V.tensor_copy(stat1[:, 0:2, :], src[0:TT, 0:4].rearrange("p (c s) -> p c s", s=2)))
                        stat_sb.done(V.tensor_copy(stat1[0:LASTP, 2, :], src[0:LASTP, 4:6]))
                    for c in range(TILES):
                        rows = TT if c < 2 else LASTP
                        for n, p in images(slot, par, s, AT["yn"][c]):
                            y_pe.wait(dve, n, c + 1)
                            rstd1_pool.wait(dve, n, 5)
                            xn_pe.wait(dve, n - 1, 2)
                            y_sb.done(V.scalar_tensor_tensor(out=yxn[0:rows, c, :], in0=place("y", c)[0:rows, 0:E],
                                                             scalar=rstd1[0:rows, c:c + 1], in1=c0b[0:rows, :], op0=ALU.mult, op1=ALU.add))
                        for n, p in images(slot, par, s, AT["st2"][c]):
                            y_sb.wait(dve, n, c + 1)
                            st2.done(V.bn_stats(bn2[0:rows, c, :], yxn[0:rows, c, :]))
                        for n, p in images(slot, par, s, AT["mv2"]):
                            rs2_pool.wait(dve, n - 1, 2)
                            aggregate(n, c, bn2, st2, mv2, mv2_sb, rows)
                    for c in range(TILES):
                        rows = TT if c < 2 else LASTP
                        for n, p in images(slot, par, s, AT["hg"][c]):
                            mv2_sb.wait(dve, n, c + 1)
                            hg.done(V.scalar_tensor_tensor(out=yxn[0:rows, c, :], in0=yxn[0:rows, c, :], scalar=mv2[0:rows, c, 0:1],
                                                           in1=g2b[0:rows, :], op0=ALU.subtract, op1=ALU.mult))
                        for n, p in images(slot, par, s, AT["h"][c]):
                            rs2_pool.wait(dve, n, 2)
                            hb_sb.wait(dve, n - 1, 1)
                            xn_sb.wait(dve, n - 1, 3)
                            hg.wait(dve, n, c + 1)
                            h_sb.done(V.scalar_tensor_tensor(out=h[0:rows, c, :], in0=yxn[0:rows, c, :], scalar=rs2[0:rows, c:c + 1],
                                                             in1=b2b[0:rows, :], op0=ALU.mult, op1=ALU.add))
                    for c in range(TILES):
                        for n, p in images(slot, par, s, AT["st3"][c]):
                            h_sb.wait(dve, n, c + 1)
                            if c == 2:
                                txt_in.wait(dve, n, 1)
                            st3.done(V.bn_stats(bn3[:, c, :], h[:, c, :]))
                        for n, p in images(slot, par, s, AT["mv3"]):
                            aggregate(n, c, bn3, st3, mv3, mv3_sb)
                    for k in range(2):
                        for n, p in images(slot, par, s, AT["xnl"][k]):
                            xn_hi.wait(dve, n, k + 1)
                            xn_lo.done(V.tensor_tensor(xnT[:, 1, k, 0:T], place("xt", k)[:, 0:T], xnT[:, 0, k, 0:T].bitcast(F32), ALU.subtract))
                    for job in range(6):
                        for n, p in images(slot, par, s, AT["qb"][job]):
                            c, half = job // 2, job % 2
                            qkv_pe.wait(dve, n, job + 1)
                            if half == 0:
                                qkv_out[c].wait(dve, n - 1, 1)
                            qkv_sb.done(V.tensor_tensor(qkvt[:, c, NQ * half:NQ * half + NQ], place("qkv", job)[0:TT, 0:NQ],
                                                        bqkv[0:TT, :, :].rearrange("p i j -> p (i j)")[:, NQ * half:NQ * half + NQ], ALU.add))
                    for k in range(2):
                        for n, p in images(slot, par, s, AT["onl"][k]):
                            on_hi.wait(dve, n, k + 1)
                            on_lo.done(V.tensor_tensor(onT[:, 1, k, 0:T], place("ont", k)[:, 0:T], onT[:, 0, k, 0:T].bitcast(F32), ALU.subtract))
                    for c in range(TILES):
                        for n, p in images(slot, par, s, AT["h2"][c]):
                            wo_pe.wait(dve, n, c + 1)
                            hb_sb.wait(dve, n, 1)
                            if c == 0:
                                out_dma.wait(dve, n - 2, 3)
                            h2_sb.done(V.tensor_tensor(h2[:, p, c, :], place("wo", c)[0:TT, 0:E], hb[:, p, c, :], ALU.add))
                        for n, p in images(slot, par, s, AT["st4"][c]):
                            h2_sb.wait(dve, n, c + 1)
                            st4.done(V.bn_stats(bn4[:, c, :], h2[:, p, c, :]))
                        for n, p in images(slot, par, s, AT["mv4"]):
                            rs4_pool.wait(dve, n - 1, 4)
                            aggregate(n, c, bn4, st4, mv4, mv4_sb)
                    for j in range(4):
                        for n, p in images(slot, par, s, AT["mix"][j]):
                            w, k = j // 2, j % 2
                            d_sb.wait(dve, n, k + 1)
                            mix_lo.wait(dve, n - 1, j + 1)
                            mix_sb.done(V.scalar_tensor_tensor(out=mixf[:, j, 0:T], in0=dT[:, k, 0:T], scalar=mus[:, w, k:k + 1],
                                                               in1=zT[:, k, 0:T], op0=ALU.mult, op1=ALU.add))
                    for c in range(TILES):
                        for n, p in images(slot, par, s, AT["rv"][c]):
                            val_pe.wait(dve, n, c + 1)
                            r_tanh.wait(dve, n, c + 1)
                            out_sb.wait(dve, n - 1, c + 1)
                            rv_sb.done(V.scalar_tensor_tensor(out=rv[:, c, :], in0=r[:, c, :], scalar=1.0,
                                                              in1=place("val", c)[0:TT, 0:E], op0=ALU.add, op1=ALU.mult))

            slots(dve, body)

        @block.scalar
        def _(act):
            A = nc.scalar
            act.wait_ge(ready, 1)

            def body(slot, par):
                for s in range(SLOT):
                    for t in range(GT):
                        for n, p in images(slot, par, s, AT["spread"][t]):
                            if t == 0:
                                qkv_in.wait(act, n, 3)
                                av_pe.wait(act, n - 1, 3)
                            kvb_sb.done(A.activation(kvb[:, :, t, 0:2 * HD], qkv[:, :, HD:QKV], ACT.Copy, scale=tokmask[:, t:t + 1]))
                    for part, (g0, g1) in enumerate(PARTS):
                        r0, r1 = g0 // 4, g1 // 4
                        for n, p in images(slot, par, s, AT["exp"][part]):
                            s_sub.wait(act, n, part + 1)
                            p_exp.done(A.activation(probs[:, r0:r1, :, :], probs[:, r0:r1, :, :], ACT.Exp))
                        for n, p in images(slot, par, s, AT["ptc"][part]):
                            pt_pe.wait(act, n, part + 1)
                            av_pe.wait(act, n - 1, part + 1)
                            pt_sb.done(A.activation(probsT[:, r0:r1, :], place("pt", part)[:, 0:128 * (r1 - r0)], ACT.Copy))
                    for job, (w0, w1) in enumerate(XCUT):
                        for n, p in images(slot, par, s, AT["xcols"][job]):
                            if job == 0:
                                x_in.wait(act, n, 2)
                                x_tr.wait(act, n - 1, 3)
                            x_cols.done(A.activation(
                                xcols[:, 128 * w0:128 * w1].rearrange("p (w r q) -> p w r q", r=HALF, q=PS),
                                xim[:, :].rearrange("p (r w q) -> p w r q", r=HALF, q=PS)[:, w0:w1, :, :], ACT.Copy))
                        for n, p in images(slot, par, s, AT["xh"][job]):
                            x_tr.wait(act, n, job + 1)
                            if job == 0:
                                tok_pe.wait(act, n - 1, 2)
                            src = place("x", job)[:, 0:XROWS * (w1 - w0)].rearrange("p (w j) -> p j w", j=XROWS)
                            x_hi.done(A.activation(xT[:, 0, :, w0:w1], src, ACT.Copy))
                    for m in range(2):
                        for n, p in images(slot, par, s, AT["yt"][m]):
                            tok_pe.wait(act, n, m + 1)
                            y_pe.wait(act, n - 1, 3)
                            yT_sb.done(A.activation(yT[:, m, :], place("tok", m)[:, 0:PATCHES], ACT.Copy))
                    for c in range(TILES):
                        for n, p in images(slot, par, s, AT["xn"][c]):
                            rs3_pool.wait(act, n, 4)
                            st2.wait(act, n, 3)
                            h_sb.wait(act, n, 3)
                            txt_in.wait(act, n, 1)
                            xn_pe.wait(act, n - 1, 2)
                            xn_sb.done(A.activation(yxn[:, c, :], h[:, c, :], ACT.Identity, bias=nm3[:, c:c + 1], scale=rs3[:, c:c + 1]))
                    for k in range(2):
                        for n, p in images(slot, par, s, AT["xnh"][k]):
                            xn_pe.wait(act, n, k + 1)
                            qkv_pe.wait(act, n - 1, 6)
                            xn_hi.done(A.activation(xnT[:, 0, k, 0:T], place("xt", k)[:, 0:T], ACT.Copy))
                    for k in range(2):
                        for n, p in images(slot, par, s, AT["onh"][k]):
                            on_pe.wait(act, n, k + 1)
                            wo_pe.wait(act, n - 1, 3)
                            on_hi.done(A.activation(onT[:, 0, k, 0:T], place("ont", k)[:, 0:T], ACT.Copy))
                    for c in range(TILES):
                        for n, p in images(slot, par, s, AT["z"][c]):
                            rs4_pool.wait(act, n, 4)
                            z_pe.wait(act, n - 1, 2)
                            z_sb.done(A.activation(z[:, c, :], h2[:, p, c, :], ACT.Identity, bias=nm4[:, c:c + 1], scale=rs4[:, c:c + 1]))
                    for k in range(2):
                        for n, p in images(slot, par, s, AT["ztc"][k]):
                            z_pe.wait(act, n, k + 1)
                            mix_sb.wait(act, n - 1, 4)
                            zT_sb.done(A.activation(zT[:, k, 1:TP], place("zt", k)[:, 0:T], ACT.Copy))
                    for j in range(4):
                        for n, p in images(slot, par, s, AT["mixh"][j]):
                            w, k = j // 2, j % 2
                            mix_sb.wait(act, n, j + 1)
                            (r_pe if w else k_pe).wait(act, n - 1, 3 if w else 2)
                            mix_hi.done(A.activation(mixp[:, w, 0, k, :], mixf[:, j, :], ACT.Copy))
                    for m in range(2):
                        for n, p in images(slot, par, s, AT["kr"][m]):
                            k_pe.wait(act, n, m + 1)
                            ka_sb.wait(act, n - 1, m + 1)
                            kr_sb.done(A.activation(kr[:, m, 0:T], place("k", m)[:, 0:T], ACT.Relu))
                        for n, p in images(slot, par, s, AT["kah"][m]):
                            ka_sb.wait(act, n, m + 1)
                            val_pe.wait(act, n - 1, 3)
                            ka_hi.done(A.activation(kaT[:, 0, m, :], kaf[:, m, :], ACT.Copy))
                    for c in range(TILES):
                        for n, p in images(slot, par, s, AT["rt"][c]):
                            r_pe.wait(act, n, c + 1)
                            rv_sb.wait(act, n - 1, 3)
                            r_tanh.done(A.activation(r[:, c, :], place("r", c)[0:TT, 0:E], ACT.Tanh, scale=0.5))

            slots(act, body)

        @block.tensor
        def _(pe):
            mm, tr = nc.tensor.matmul, nc.tensor.transpose

            def product(psum, left, right):
                terms = [(a, b, k) for k in range(2) for a, b in ((0, 0), (0, 1), (1, 0))]
                for t, (a, b, k) in enumerate(terms):
                    last = mm(psum, left(a, k), right(b, k), start=t == 0, stop=t == len(terms) - 1)
                return last

            def turn(slot, kind, j):
                same = [job for job in JOBS if BANK[job[0]][job[1]] == BANK[kind][j]]
                at = same.index((kind, j)) - 1
                while True:
                    if at < 0:
                        at, slot = at + len(same), slot - 1
                    kind, j = same[at]
                    n = slot - step_of(kind, j) // SLOT
                    if not isinstance(slot, int) or 0 <= n < IMAGES:
                        return READ[kind].wait(pe, n, 2 if kind == "stat" else j + 1)
                    if slot < 0:
                        return
                    at -= 1

            pe.wait_ge(raw_in, RAWS * 16)
            pe.wait_ge(prep_pool, 6)
            pe.wait_ge(prep_dve, KCH)
            for ch in range(KCH):
                last = mm(banks[0][:, 0:E], c0rep[:, ch, :], raw[:, ch, :], start=ch == 0, stop=ch == KCH - 1)
            last.then_inc(prep_pe, 1)
            pe.wait_ge(prep_dve, 2 * KCH + 1)
            for ch in range(KCH):
                last = mm(banks[2][:, 0:E], ones[:, :], raw[:, ch, :], start=ch == 0, stop=ch == KCH - 1)
            last.then_inc(prep_pe, 1)
            for n in range(len(WEIGHTS)):
                if n >= 2:
                    pe.wait_ge(prep_dve, DVE_TOK + 4 * (n - 1))
                for k in range(2):
                    for a in range(2):
                        last = tr(banks[n % 2][:, E * k + 128 * a:E * k + 128 * a + 128], rawsq[:, n, a, 128 * k:128 * k + 128], ident[:, :])
                last.then_inc(prep_pe, 1)
            pe.wait_ge(ready, 1)

            def body(slot, par):
                for s in range(SLOT):
                    for part, (g0, g1) in enumerate(PARTS):
                        for n, p in images(slot, par, s, AT["s"][part]):
                            if part == 0:
                                kvb_sb.wait(pe, n, 8)
                            turn(slot, "s", part)
                            for g in range(g0, g1):
                                row, j = (g - g0) // 4, g % 4
                                last = mm(place("s", part)[32 * j:32 * j + 32, 128 * row:128 * row + 128], qkv[:, g, 0:2 * HD],
                                          kvb[:, g, :, 0:HD], start=True, stop=True)
                            s_pe.done(last)
                        for n, p in images(slot, par, s, AT["pt"][part]):
                            p_exp.wait(pe, n, part + 1)
                            turn(slot, "pt", part)
                            for row in range((g1 - g0) // 4):
                                last = tr(place("pt", part)[:, 128 * row:128 * row + 128],
                                          probs[:, g0 // 4 + row, :, :].rearrange("p t k -> p (t k)"), ident[:, :])
                            pt_pe.done(last)
                        for n, p in images(slot, par, s, AT["av"][part]):
                            pt_sb.wait(pe, n, part + 1)
                            turn(slot, "av", part)
                            for g in range(g0, g1):
                                row, j = (g - g0) // 4, g % 4
                                last = mm(place("av", part)[32 * j:32 * j + 32, AVW * row:AVW * row + AVW], probsT[:, g // 4, 32 * j:32 * j + 32],
                                          kvb[:, g, :, HD:2 * HD + 1], start=True, stop=True)
                            av_pe.done(last)
                    for job, (w0, w1) in enumerate(XCUT):
                        for n, p in images(slot, par, s, AT["x"][job]):
                            x_cols.wait(pe, n, job + 1)
                            turn(slot, "x", job)
                            for w in range(w0, w1):
                                last = tr(place("x", job)[:, XROWS * (w - w0):XROWS * (w - w0) + XROWS],
                                          xcols[:, 128 * w:128 * w + 128], ident[0:XROWS, 0:XROWS])
                            x_tr.done(last)
                    for m in range(2):
                        for n, p in images(slot, par, s, AT["tok"][m]):
                            x_lo.wait(pe, n, 3)
                            turn(slot, "tok", m)
                            terms = [(a, b, ch) for ch in range(KCH) for a, b in ((0, 0), (0, 1), (1, 0))]
                            for t, (a, b, ch) in enumerate(terms):
                                last = mm(place("tok", m)[:, 0:PATCHES], wtok[:, a, ch, 128 * m:128 * m + 128],
                                          xT[:, b, GRID * ch:GRID * ch + GRID, :], start=t == 0, stop=t == len(terms) - 1)
                            tok_pe.done(last)
                    for n, p in images(slot, par, s, AT["stat"]):
                        turn(slot, "stat", 0)
                        sums_pool.wait(pe, n, 8)
                        for c in range(TILES):
                            rows = TT if c < 2 else LASTP
                            for v in range(2):
                                last = mm(place("stat", 0)[0:rows, 2 * c + v:2 * c + v + 1],
                                          xspread[:, v, :, :].rearrange("p i w -> p (i w)")[:, TT * c:TT * c + rows],
                                          ones[0:XROWS, 0:1], start=True, stop=True)
                        stat_pe.done(last)
                    for c in range(TILES):
                        rows = TT if c < 2 else LASTP
                        for n, p in images(slot, par, s, AT["y"][c]):
                            yT_sb.wait(pe, n, 2)
                            turn(slot, "y", c)
                            for m in range(2):
                                last = tr(place("y", c)[0:rows, 128 * m:128 * m + 128], yT[:, m, TT * c:TT * c + rows], ident[:, :])
                            y_pe.done(last)
                    for k in range(2):
                        for n, p in images(slot, par, s, AT["xt"][k]):
                            xn_sb.wait(pe, n, 3)
                            turn(slot, "xt", k)
                            for c in range(TILES):
                                last = tr(place("xt", k)[:, TT * c:TT * c + TT], yxn[:, c, 128 * k:128 * k + 128], ident[0:TT, 0:TT])
                            xn_pe.done(last)
                    for job in range(6):
                        for n, p in images(slot, par, s, AT["qkv"][job]):
                            c, half = job // 2, job % 2
                            xn_lo.wait(pe, n, 2)
                            turn(slot, "qkv", job)
                            qkv_pe.done(product(place("qkv", job)[0:TT, 0:NQ], lambda a, k: xnT[:, a, k, TT * c:TT * c + TT],
                                                lambda b, k: wqkv[:, b, k, NQ * half:NQ * half + NQ]))
                    for k in range(2):
                        for n, p in images(slot, par, s, AT["ont"][k]):
                            on_in.wait(pe, n, 1)
                            turn(slot, "ont", k)
                            for c in range(TILES):
                                last = tr(place("ont", k)[:, TT * c:TT * c + TT], on[:, c, 128 * k:128 * k + 128], ident[0:TT, 0:TT])
                            on_pe.done(last)
                    for c in range(TILES):
                        for n, p in images(slot, par, s, AT["wo"][c]):
                            on_lo.wait(pe, n, 2)
                            turn(slot, "wo", c)
                            wo_pe.done(product(place("wo", c)[0:TT, 0:E], lambda a, k: onT[:, a, k, TT * c:TT * c + TT],
                                               lambda b, k: wmat["woT"][:, b, k, :]))
                    for k in range(2):
                        for n, p in images(slot, par, s, AT["zt"][k]):
                            z_sb.wait(pe, n, 3)
                            turn(slot, "zt", k)
                            for c in range(TILES):
                                last = tr(place("zt", k)[:, TT * c:TT * c + TT], z[:, c, 128 * k:128 * k + 128], ident[0:TT, 0:TT])
                            z_pe.done(last)
                    for m in range(2):
                        for n, p in images(slot, par, s, AT["k"][m]):
                            mix_lo.wait(pe, n, 2)
                            turn(slot, "k", m)
                            k_pe.done(product(place("k", m)[:, 0:TP], lambda a, k: wmat["wkfT"][:, a, k, 128 * m:128 * m + 128],
                                              lambda b, k: mixp[:, 0, b, k, :]))
                    for c in range(TILES):
                        for n, p in images(slot, par, s, AT["r"][c]):
                            mix_lo.wait(pe, n, 4)
                            turn(slot, "r", c)
                            r_pe.done(product(place("r", c)[0:TT, 0:E], lambda a, k: mixp[:, 1, a, k, TT * c:TT * c + TT],
                                              lambda b, k: wmat["wrT"][:, b, k, :]))
                        for n, p in images(slot, par, s, AT["val"][c]):
                            ka_lo.wait(pe, n, 2)
                            turn(slot, "val", c)
                            val_pe.done(product(place("val", c)[0:TT, 0:E], lambda a, k: kaT[:, a, k, TT * c:TT * c + TT],
                                                lambda b, k: wmat["wvfT"][:, b, k, :]))

            slots(pe, body)


INPUTS = ["x", "txt", "L0_tok_ln1_g", "L0_tok_ln1_b", "L0_tok_W", "L0_tok_b", "L0_tok_ln2_g", "L0_tok_ln2_b",
          "L0_attn_Wq", "L0_attn_bq", "L0_attn_Wk", "L0_attn_bk", "L0_attn_Wv", "L0_attn_bv", "L0_attn_Wo",
          "L0_attn_bo", "L0_ffn_W_r", "L0_ffn_W_k", "L0_ffn_W_v", "L0_ffn_mu_r", "L0_ffn_mu_k"]


def kernel(**inputs):
    import numpy as np
    import concourse.bacc as bacc
    from concourse.bass_utils import run_bass_kernel_spmd

    nc = bacc.Bacc("TRN2", target_bir_lowering=False, num_devices=1)
    arrays, args = {}, []
    for name in INPUTS:
        a = np.ascontiguousarray(inputs[name])
        arrays[f"in_{name}"] = a
        args.append(nc.dram_tensor(f"in_{name}", a.shape, mybir.dt.from_np(a.dtype), kind="ExternalInput").ap())
    args.append(nc.dram_tensor("out", (IMAGES, T, E), F32, kind="ExternalOutput").ap())
    fusion_kernel(nc, *args)
    return run_bass_kernel_spmd(nc, [arrays], core_ids=[0]).results[0]["out"]
```
